# Optimizing a Trainium2 kernel written in Bass

```python
import numpy as np
import jax
import jax.numpy as jnp

def _softmax(x, axis=-1):
    return jax.nn.softmax(x, axis=axis)

def _gelu(x):
    return jax.nn.gelu(x, approximate=True)

def _silu(x):
    return jax.nn.silu(x)

def _sigmoid(x):
    return jax.nn.sigmoid(x)

def _layernorm(x, axis=-1, eps=1e-05):
    m = jnp.mean(x, axis=axis, keepdims=True)
    v = jnp.var(x, axis=axis, keepdims=True)
    return (x - m) / jnp.sqrt(v + eps)

def _scatter_add(tgt, idx, src, axis=0):
    return tgt.at[idx].add(src)

def _segment_sum(src, seg, n):
    return jax.ops.segment_sum(src, seg, n)
kernel_name = 'mk_macaron_d1_jaxref_r8_023bc1'

def setup_inputs(seed: int=0):
    np.random.seed(seed)
    _w = jnp.asarray

    def _L0_attn_setup():
        import jax, jax.numpy as jnp
        import numpy as np
        KEY_DIM = 16
        key = jax.random.key(seed)
        k1, k2, k3, k4, k5 = jax.random.split(key, 5)
        B, N, D, H, KD, VD = (2, 256, 128, 16, 16, 64)
        return {'x': jax.random.normal(k1, (B, N, D), dtype=jnp.float32), 'query_proj': jax.random.normal(k2, (H, KD, D), dtype=jnp.float32) * 0.02, 'key_proj': jax.random.normal(k3, (H, KD, D), dtype=jnp.float32) * 0.02, 'value_proj': jax.random.normal(k4, (H, VD, D), dtype=jnp.float32) * 0.02, 'output_proj': jax.random.normal(k5, (D, H, VD), dtype=jnp.float32) * 0.02}
    _L0_attn_in = _L0_attn_setup()

    def _L0_ffn_setup():
        import jax, jax.numpy as jnp
        import numpy as np
        NS, L, H = (8, 256, 128)
        M, E, K = (512, 8, 2)
        EPS = 1e-09
        key = jax.random.key(seed)
        ks = jax.random.split(key, 5)
        s = 0.02
        return {'x': jax.random.normal(ks[0], (NS, L, H), jnp.float32), 'Wr': jax.random.normal(ks[1], (H, E), jnp.float32) * s, 'br': jnp.zeros((E,), jnp.float32), 'W1': jax.random.normal(ks[2], (E, H, M), jnp.float32) * s, 'b1': jnp.zeros((E, M), jnp.float32), 'W2': jax.random.normal(ks[3], (E, M, H), jnp.float32) * s, 'b2': jnp.zeros((E, H), jnp.float32)}
    _L0_ffn_in = _L0_ffn_setup()
    _d = {'L0_attn_x': _L0_attn_in['x'], 'L0_attn_query_proj': _L0_attn_in['query_proj'], 'L0_attn_key_proj': _L0_attn_in['key_proj'], 'L0_attn_value_proj': _L0_attn_in['value_proj'], 'L0_attn_output_proj': _L0_attn_in['output_proj'], 'L0_ffn_Wr': _L0_ffn_in['Wr'], 'L0_ffn_br': _L0_ffn_in['br'], 'L0_ffn_W1': _L0_ffn_in['W1'], 'L0_ffn_b1': _L0_ffn_in['b1'], 'L0_ffn_W2': _L0_ffn_in['W2'], 'L0_ffn_b2': _L0_ffn_in['b2']}
    _x0 = _d['L0_attn_x']
    _d['L0_attn_x'] = jax.random.normal(jax.random.fold_in(jax.random.key(seed), 1), (2, 1024, 128), dtype=_x0.dtype)
    del _x0
    return _d

def reference(L0_attn_x, L0_attn_query_proj, L0_attn_key_proj, L0_attn_value_proj, L0_attn_output_proj, L0_ffn_Wr, L0_ffn_br, L0_ffn_W1, L0_ffn_b1, L0_ffn_W2, L0_ffn_b2):

    def _L0_attn_ref(x, query_proj, key_proj, value_proj, output_proj):
        import jax, jax.numpy as jnp
        import numpy as np
        KEY_DIM = 16
        q = jnp.einsum('bnd,hkd->bnhk', x, query_proj)
        k = jnp.einsum('bnd,hkd->bnhk', x, key_proj)
        v = jnp.einsum('bnd,hvd->bnhv', x, value_proj)
        sim = jnp.einsum('bnkh,bmhk->bnhm', q, k)
        scale = jnp.asarray(1.0 / np.sqrt(KEY_DIM), dtype=sim.dtype)
        attn = jax.nn.softmax(sim * scale, axis=1)
        o = jnp.einsum('bnhm,bmhv->bnhv', attn, v)
        return jnp.einsum('bnhv,dhv->bnd', o, output_proj)

    def _L0_ffn_ref(x, Wr, br, W1, b1, W2, b2):
        import jax, jax.numpy as jnp
        import numpy as np
        NS, L, H = (8, 256, 128)
        M, E, K = (512, 8, 2)
        EPS = 1e-09
        ns, seq, h = x.shape
        flat = x.reshape(-1, h)
        logits = flat @ Wr + br
        probs = jax.nn.softmax(logits, axis=-1)
        vals, idx = jax.lax.top_k(probs, K)
        w = vals / (jnp.sum(vals, axis=-1, keepdims=True) + EPS)
        out_acc = jnp.zeros_like(flat)
        weight_acc = jnp.zeros((flat.shape[0],), flat.dtype)
        for e in range(E):
            we = jnp.sum(w * (idx == e), axis=-1)
            hmid = jax.nn.gelu(flat @ W1[e] + b1[e], approximate=False)
            y = hmid @ W2[e] + b2[e]
            out_acc = out_acc + we[:, None] * y
            weight_acc = weight_acc + we
        out = out_acc / (weight_acc[:, None] + EPS)
        return out.reshape(ns, seq, h)
    x = L0_attn_x
    x = x + 0.5 * _L0_ffn_ref(_layernorm(x, axis=-1), L0_ffn_Wr, L0_ffn_br, L0_ffn_W1, L0_ffn_b1, L0_ffn_W2, L0_ffn_b2)
    x = x + _L0_attn_ref(_layernorm(x, axis=-1), L0_attn_query_proj, L0_attn_key_proj, L0_attn_value_proj, L0_attn_output_proj)
    x = x + 0.5 * _L0_ffn_ref(_layernorm(x, axis=-1), L0_ffn_Wr, L0_ffn_br, L0_ffn_W1, L0_ffn_b1, L0_ffn_W2, L0_ffn_b2)
    return x

_drawn_inputs = setup_inputs


def setup_inputs(seed=0):
    import zlib

    import numpy as np

    out = dict(_drawn_inputs(seed))
    spreads = {'L0_ffn_br': (0.0, 0.1), 'L0_ffn_b1': (0.0, 0.469), 'L0_ffn_b2': (0.0, 0.1)}
    factors = {'L0_attn_query_proj': 8.0,
     'L0_attn_key_proj': 8.0,
     'L0_attn_value_proj': 8.0,
     'L0_attn_output_proj': 8.0}
    for name, (base, spread) in spreads.items():
        noise = np.random.default_rng([zlib.crc32(name.encode()), seed]).standard_normal(out[name].shape)
        drawn = base * np.exp(spread * noise) if base else spread * noise
        out[name] = jnp.asarray(drawn.astype(out[name].dtype))
    for name, factor in factors.items():
        out[name] = (out[name] * factor).astype(out[name].dtype)
    return out
```

```python
import concourse.bass as bass
from concourse import mybir
from contextlib import ExitStack

F32 = mybir.dt.float32
F32R = mybir.dt.float32r
ALU = mybir.AluOpType
ACT = mybir.ActivationFunctionType
AX = mybir.AxisListType

P = 128
D = 128
B, N = 2, 1024
TOK = B * N
NT = TOK // P
GR = TOK // 512
TPG = NT // GR
E, M = 8, 512
MC = M // P
H, KD, VD = 16, 16, 64
PAIRS = H // 2
QUADS = H // 4
MT = N // P
LN_EPS = 1e-5
EPS = 1e-9
SCALE = float(KD) ** -0.5
PARTS = 4

C_ID, C_QM, C_KM, C_TIE = 0, P, P + 1, P + 2
C_W = P + 2 + E * E


def macaron_kernel(nc, x, cst, wqk, wv, wo, wr, br, w1, b1, w2, b2, out):
    ctx = ExitStack()
    with ctx:
        def sem(name):
            return ctx.enter_context(nc.semaphore(name))

        def sb(name, shape, dt, stack=ctx):
            return stack.enter_context(nc.sbuf_tensor(name, shape, dt))

        ps = ctx.enter_context(nc.psum_tensor("ps", [P, 8 * 512], F32))

        def bank(b, n=1):
            return ps[:, b * 512:(b + n) * 512]

        xt = sb("xt", [P, NT, D], F32)
        xhi = sb("xhi", [P, TOK], F32R)
        xlo = sb("xlo", [P, TOK], F32R)
        xn = sb("xn", [P, 2, TPG, D], F32)
        consts = sb("consts", [P, C_W], F32)
        ident = consts[:, C_ID:C_ID + P]
        qmask = consts[:, C_QM:C_QM + 1]
        kmask = consts[:, C_KM:C_KM + 1]
        tie = consts[:, C_TIE:C_TIE + E * E]
        stats = sb("stats", [P, NT, 6], F32)
        mv = sb("mv", [P, NT, 2], F32)
        rstd = sb("rstd", [P, NT], F32)
        mark = sb("mark", [P, 14], F32)
        mhalf = sb("mhalf", [P, TPG], F32)
        wr_sb = sb("wr_sb", [P, E], F32)
        br_sb = sb("br_sb", [P, E], F32)
        b1_sb = sb("b1_sb", [P, 2, MC], F32)
        b2_sb = sb("b2_sb", [P, E], F32)

        ffn = ExitStack()
        xf = sb("xf", [P, TOK], F32, ffn)
        acc = sb("acc", [P, TOK], F32, ffn)
        w1raw = sb("w1raw", [P, 2, M], F32, ffn)
        w2raw = sb("w2raw", [P, 2, MC * D], F32, ffn)
        w1hi = sb("w1hi", [P, 2, M], F32R, ffn)
        w1lo = sb("w1lo", [P, 2, M], F32R, ffn)
        w2hi = sb("w2hi", [P, 2, MC * D], F32R, ffn)
        w2lo = sb("w2lo", [P, 2, MC * D], F32R, ffn)
        gb = sb("gb", [P, 2, TOK], F32, ffn)
        hf = sb("hf", [P, MC, 512], F32, ffn)
        hhi = sb("hhi", [P, 2, MC, 512], F32R, ffn)
        hlo = sb("hlo", [P, 2, MC, 512], F32R, ffn)
        ysc = sb("ysc", [P, 2, 512], F32, ffn)
        pr = sb("pr", [P, NT, E], F32, ffn)
        gw = sb("gw", [P, NT, E], F32, ffn)
        rank = sb("rank", [P, NT, E], F32, ffn)
        col = sb("col", [P, NT], F32, ffn)
        rcol = sb("rcol", [P, NT], F32, ffn)
        gte = sb("gte", [P, E, NT], F32, ffn)
        gT = sb("gT", [P, P], F32, ffn)
        cge = sb("cge", [P, NT, E, E], F32, ffn)
        cgt = sb("cgt", [P, NT, E, E], F32, ffn)
        ffn.close()

        att = ExitStack()
        V = sb("V", [P, NT, H * VD], F32, att)
        att_wv = ExitStack()
        wvraw = sb("wvraw", [P, H * VD], F32, att_wv)
        wvhi = sb("wvhi", [P, H * VD], F32R, att_wv)
        wvlo = sb("wvlo", [P, H * VD], F32R, att_wv)
        att_wv.close()
        RING = 4
        ef = sb("ef", [P, RING, N], F32, att)
        ehi = sb("ehi", [P, RING, N], F32R, att)
        elo = sb("elo", [P, RING, N], F32R, att)
        qs = sb("qs", [P, 2, N], F32R, att)
        ks = sb("ks", [P, 2, 2, N], F32R, att)
        cut = sb("cut", [P, N], F32R, att)
        vs = sb("vs", [P, RING, 2 * VD], F32R, att)
        oT = sb("oT", [P, N], F32, att)
        wqraw = sb("wqraw", [P, 2, 2 * P], F32, att)
        wqhi = sb("wqhi", [P, 2, 2 * P], F32R, att)
        wqlo = sb("wqlo", [P, 2, 2 * P], F32R, att)
        wo_sb = sb("wo_sb", [P, 4, D], F32, att)
        nmax = sb("nmax", [P, 8], F32, att)
        esum = sb("esum", [P, 8], F32, att)
        rsum = sb("rsum", [P, 8], F32, att)
        zero = sb("zero", [P, 512], F32R, att)
        aT = sb("aT", [P, TOK], F32, att)
        att.close()

        gd = [nc.dram_tensor(f"gates{f}", [P, P], F32, kind="Internal").ap() for f in range(2)]

        x_v = x.rearrange("b n d -> (b n) d").rearrange("(g t p) d -> g p t d", g=GR, p=P)
        out_v = out.rearrange("b n d -> (b n) d").rearrange("(g t p) d -> g p t d", g=GR, p=P)

        s_x = [sem(f"s_x{g}") for g in range(GR)]
        s_cst = sem("s_cst")
        s_fill = sem("s_fill")
        s_out = sem("s_out")

        class Norm:
            def __init__(self, k, src):
                self.k, self.src = k, src
                self.back = sem(f"n{k}_back")
                self.res = sem(f"n{k}_res")
                self.st = sem(f"n{k}_st")
                self.mv = sem(f"n{k}_mv")
                self.eps = sem(f"n{k}_eps")
                self.rstd = sem(f"n{k}_rstd")
                self.xn = sem(f"n{k}_xn")
                self.fwd = sem(f"n{k}_fwd")
                self.x32 = sem(f"n{k}_x32")
                self.hi = sem(f"n{k}_hi")
                self.lo = sem(f"n{k}_lo")

        norms = [Norm(0, None), Norm(1, acc), Norm(2, aT), Norm(3, acc)]

        def back_pe(pe, n, g):
            if g >= 2:
                pe.wait_ge(n.res, g - 1)
            for t in range(TPG):
                at = (g * TPG + t) * P
                last = nc.tensor.transpose(bank(g % 2)[:, t * P:(t + 1) * P], n.src[:, at:at + P], ident)
            last.then_inc(n.back, 1)

        def residual_dve(dve, n, g):
            dve.wait_ge(n.back, g + 1)
            xg = xt[:, g * TPG:(g + 1) * TPG, :]
            nc.vector.tensor_tensor(xg, xg, bank(g % 2).rearrange("p (t d) -> p t d", d=D), ALU.add).then_inc(n.res, 1)

        def norm_pe(pe, n):
            if n.src is not None:
                for g in range(GR):
                    back_pe(pe, n, g)
            for g in range(GR):
                pe.wait_ge(n.xn, g + 1)
                if g >= 2:
                    pe.wait_ge(n.lo, g - 1)
                for t in range(TPG):
                    last = nc.tensor.transpose(bank(6 + g % 2)[:, t * P:(t + 1) * P], xn[:, g % 2, t, :], ident)
                last.then_inc(n.fwd, 1)

        def norm_act(act, n):
            for g in range(GR):
                cols = slice(g * 512, (g + 1) * 512)
                act.wait_ge(n.fwd, g + 1)
                if n.k != 1:
                    nc.scalar.activation(xf[:, cols], bank(6 + g % 2), ACT.Copy).then_inc(n.x32, 1)
                nc.scalar.activation(xhi[:, cols], bank(6 + g % 2), ACT.Copy).then_inc(n.hi, 1)

        def norm_pool(pool, n):
            for g in range(GR):
                r = rstd[:, g * TPG:(g + 1) * TPG]
                pool.wait_ge(n.mv, g + 1)
                nc.gpsimd.tensor_scalar(r, mv[:, g * TPG:(g + 1) * TPG, 1], LN_EPS, None, ALU.add).then_inc(n.eps, 1)
                pool.wait_ge(n.eps, g + 1)
                nc.gpsimd.tensor_tensor(r, r, mhalf[:, :], ALU.pow).then_inc(n.rstd, 1)

        def norm_dve(dve, n):
            def statistics(g):
                if n.src is None:
                    dve.wait_ge(s_x[g], 16)
                else:
                    residual_dve(dve, n, g)
                    dve.wait_ge(n.res, g + 1)
                for t in range(g * TPG, (g + 1) * TPG):
                    last = nc.vector.bn_stats(stats[:, t, :], xt[:, t, :])
                last.then_inc(n.st, 1)
                dve.wait_ge(n.st, g + 1)
                for t in range(g * TPG, (g + 1) * TPG):
                    last = nc.vector.bn_aggr(mv[:, t, :], stats[:, t, :])
                last.then_inc(n.mv, 1)

            def scaled(g):
                dve.wait_ge(n.rstd, g + 1)
                if g >= 2:
                    dve.wait_ge(n.fwd, g - 1)
                for t in range(TPG):
                    a = g * TPG + t
                    last = nc.vector.tensor_scalar(xn[:, g % 2, t, :], xt[:, a, :], mv[:, a, 0:1], rstd[:, a:a + 1],
                                                   ALU.subtract, ALU.mult)
                last.then_inc(n.xn, 1)

            def low(g):
                cols = slice(g * 512, (g + 1) * 512)
                dve.wait_ge(n.hi, g + 1)
                nc.vector.tensor_tensor(xlo[:, cols], bank(6 + g % 2), xhi[:, cols].bitcast(F32),
                                        ALU.subtract).then_inc(n.lo, 1)

            for g in range(GR + 2):
                if g < GR:
                    statistics(g)
                if 0 <= g - 1 < GR:
                    scaled(g - 1)
                if g >= 2:
                    low(g - 2)

        class Ffn:
            def __init__(self, f, n):
                self.f, self.n = f, n
                self.logit = sem(f"f{f}_logit")
                self.sh = sem(f"f{f}_sh")
                self.ex = sem(f"f{f}_ex")
                self.chain = sem(f"f{f}_chain")
                self.g = sem(f"f{f}_g")
                self.gT = sem(f"f{f}_gT")
                self.gTs = sem(f"f{f}_gTs")
                self.gd = sem(f"f{f}_gd")
                self.acc0 = sem(f"f{f}_acc0")
                self.whi = sem(f"f{f}_whi")
                self.wready = sem(f"f{f}_wready")
                self.h = sem(f"f{f}_h")
                self.gelu = sem(f"f{f}_gelu")
                self.hi = sem(f"f{f}_hi")
                self.lo = sem(f"f{f}_lo")
                self.y = sem(f"f{f}_y")
                self.scaled = sem(f"f{f}_scaled")
                self.acc = sem(f"f{f}_acc")
                self.w = [sem(f"f{f}_w{u}") for u in range(2)]
                self.gb = [sem(f"f{f}_gb{u}") for u in range(2)]
                self.b1 = [sem(f"f{f}_b1{u}") for u in range(2)]

        ffns = [Ffn(0, norms[0]), Ffn(1, norms[2])]

        Y0 = S0 = A0 = 2
        L0 = 4

        def load_expert(q, F, e, u):
            q.dma_start(w1raw[:, u, :], w1[bass.ds(e, 1), :, :].rearrange("a p n -> (a p) n")).then_inc(F.w[u], 16)
            q.dma_start(w2raw[:, u, :], w2[bass.ds(e, 1), :, :].rearrange("a p n -> (a p) n")).then_inc(F.w[u], 16)

        def load_gates(q, F, e, u):
            src = gd[F.f].rearrange("a b -> (a b)").rearrange("(e n) -> e n", e=E)[bass.ds(e, 1), :]
            q.dma_start(gb[:, u, :], src.broadcast_to([P, TOK])).then_inc(F.gb[u], 16)

        def load_bias(q, F, e, u):
            q.dma_start(b1_sb[:, u, :], b1[bass.ds(e, 1), :, :].rearrange("a p n -> (a p) n")).then_inc(F.b1[u], 16)

        def ffn_sync(sp, F):
            for e in range(2):
                load_expert(sp, F, e, e)
                load_bias(sp, F, e, e)
            sp.wait_ge(F.gTs, 1)
            sp.dma_start(gd[F.f], gT[:, :]).then_inc(F.gd, 16)
            sp.wait_ge(F.gd, 16)
            for e in range(2):
                load_gates(sp, F, e, e)
            with sp.Fori(0, E // 2 - 1) as i:
                for u in range(2):
                    sp.wait_ge(F.wready, i * 2 + (u + 1))
                    load_expert(sp, F, i * 2 + (u + 2), u)
                for u in range(2):
                    sp.wait_ge(F.scaled, i * 8 + (S0 + 4 * (u + 1)))
                    load_bias(sp, F, i * 2 + (u + 2), u)
                    load_gates(sp, F, i * 2 + (u + 2), u)

        def ffn_units(eng, front, back):
            def body(i, last):
                for s in range(2 * GR):
                    if not (last and s == 2 * GR - 1):
                        front(i, s + 1)
                    back(i, s)
            front(0, 0)
            with eng.Fori(0, E // 2 - 1) as i:
                body(i, False)
            body(E // 2 - 1, True)

        def next_expert(i, s):
            return s % GR == 1 and not (isinstance(i, int) and i == E // 2 - 1 and s >= GR)

        def ffn_pe(pe, F):
            n = F.n
            for t in range(NT):
                if t % TPG == 0:
                    pe.wait_ge(n.x32, t // TPG + 1)
                last = nc.tensor.matmul(bank(5)[:, t * E:(t + 1) * E], xf[:, t * P:(t + 1) * P], wr_sb[:, :],
                                        start=True, stop=True)
            last.then_inc(F.logit, 1)
            pe.wait_ge(n.lo, GR)

            def hidden(i, s, mc):
                u, tt = (s // GR) % 2, s % GR
                if tt == 0 and mc == 0:
                    pe.wait_ge(F.wready, i * 2 + (s // GR + 1))
                if not (isinstance(i, int) and i == 0 and s == 0):
                    pe.wait_ge(F.gelu, i * 32 + (4 * s + mc - 3))
                w = slice(mc * P, (mc + 1) * P)
                cols = slice(tt * 512, (tt + 1) * 512)
                nc.tensor.matmul(bank(mc), w1lo[:, u, w], xhi[:, cols], start=True, stop=False)
                nc.tensor.matmul(bank(mc), w1hi[:, u, w], xlo[:, cols], start=False, stop=False)
                nc.tensor.matmul(bank(mc), w1hi[:, u, w], xhi[:, cols], start=False, stop=True).then_inc(F.h, 1)

            def output(i, s, mc):
                u, tt = s // GR, s % GR
                if mc == 0:
                    pe.wait_ge(F.scaled, i * 8 + (s + S0 - 1))
                pe.wait_ge(F.lo, i * 32 + (4 * s + mc + 1 + L0))
                w = slice(mc * D, (mc + 1) * D)
                y = bank(4 + s % 2)
                nc.tensor.matmul(y, w2lo[:, u, w], hhi[:, s % 2, mc, :], start=(mc == 0), stop=False)
                nc.tensor.matmul(y, w2hi[:, u, w], hlo[:, s % 2, mc, :], start=False, stop=False)
                last = nc.tensor.matmul(y, w2hi[:, u, w], hhi[:, s % 2, mc, :], start=False, stop=(mc == MC - 1))
                if mc == MC - 1:
                    last.then_inc(F.y, 1)

            for mc in range(MC):
                hidden(0, 0, mc)
            pe.wait_ge(F.g, 1)
            nc.tensor.transpose(bank(4)[:, 0:P], gte[:, :, :].rearrange("p e t -> p (e t)"), ident).then_inc(F.gT, 1)
            pe.wait_ge(F.gTs, 1)

            def body(i, last):
                for s in range(2 * GR):
                    for mc in range(MC):
                        if not (last and s == 2 * GR - 1):
                            hidden(i, s + 1, mc)
                        output(i, s, mc)
            with pe.Fori(0, E // 2 - 1) as i:
                body(i, False)
            body(E // 2 - 1, True)

        def ffn_act(act, F):
            act.wait_ge(F.sh, 1)
            nc.scalar.activation(pr[:, :, :], pr[:, :, :], ACT.Exp).then_inc(F.ex, 1)

            def weights(i, u):
                nc.scalar.activation(w1hi[:, u, :], w1raw[:, u, :], ACT.Copy)
                nc.scalar.activation(w2hi[:, u, :], w2raw[:, u, :], ACT.Copy).then_inc(F.whi, 1)

            act.wait_ge(F.w[0], 32)
            weights(0, 0)

            def front(i, s):
                u = s // GR % 2
                if s % GR == 0:
                    act.wait_ge(F.b1[u], i * 16 + (s // (2 * GR) + 1) * 16)
                for mc in range(MC):
                    act.wait_ge(F.h, i * 32 + (4 * s + mc + 1))
                    act.wait_ge(F.lo, i * 32 + (4 * s + mc + 1))
                    nc.scalar.activation(hf[:, mc, :], bank(mc), ACT.Gelu,
                                         bias=b1_sb[:, u, mc:mc + 1]).then_inc(F.gelu, 1)

            def back(i, s):
                if next_expert(i, s):
                    u = (s // GR + 1) % 2
                    e = i * 2 + s // GR
                    act.wait_ge(F.y, e * 4 + Y0)
                    act.wait_ge(F.w[u], (i + (s // GR + 1) // 2) * 32 + 32)
                    weights(i, u)
            ffn_units(act, front, back)

        def ffn_pool(pool, F):
            nc.gpsimd.memset(acc[:, :], 0.0).then_inc(F.acc0, 1)

            def weights(u):
                nc.gpsimd.tensor_tensor(w1lo[:, u, :], w1raw[:, u, :], w1hi[:, u, :].bitcast(F32), ALU.subtract)
                nc.gpsimd.tensor_tensor(w2lo[:, u, :], w2raw[:, u, :], w2hi[:, u, :].bitcast(F32),
                                        ALU.subtract).then_inc(F.wready, 1)

            pool.wait_ge(F.whi, 1)
            weights(0)
            pool.wait_ge(F.acc0, 1)

            def body(i, last):
                for s in range(2 * GR):
                    tt = s % GR
                    pool.wait_ge(F.scaled, i * 8 + (s + 1 + S0))
                    a = acc[:, tt * 512:(tt + 1) * 512]
                    nc.gpsimd.tensor_tensor(a, a, ysc[:, s % 2, :], ALU.add).then_inc(F.acc, 1)
                    if tt == 0 and next_expert(i, s + 1):
                        pool.wait_ge(F.whi, i * 2 + (s // GR + 2))
                        weights((s // GR + 1) % 2)
            with pool.Fori(0, E // 2 - 1) as i:
                body(i, False)
            body(E // 2 - 1, True)

        def ffn_dve(dve, F):
            count = [0]

            def link(ins):
                count[0] += 1
                ins.then_inc(F.chain, 1)
                dve.wait_ge(F.chain, count[0])

            def over(t):
                return t.unsqueeze(2).broadcast_to([P, NT, E])

            dve.wait_ge(F.logit, 1)
            link(nc.vector.tensor_tensor(pr[:, :, :], bank(5)[:, 0:NT * E].rearrange("p (t e) -> p t e", e=E),
                                         br_sb[:, :].unsqueeze(1).broadcast_to([P, NT, E]), ALU.add))
            link(nc.vector.tensor_reduce(col[:, :], pr[:, :, :], AX.X, ALU.max))
            nc.vector.tensor_tensor(pr[:, :, :], pr[:, :, :], over(col[:, :]), ALU.subtract).then_inc(F.sh, 1)
            dve.wait_ge(F.ex, 1)
            link(nc.vector.tensor_reduce(col[:, :], pr[:, :, :], AX.X, ALU.add))
            link(nc.vector.reciprocal(rcol[:, :], col[:, :]))
            link(nc.vector.tensor_tensor(pr[:, :, :], pr[:, :, :], over(rcol[:, :]), ALU.mult))
            other = pr[:, :, :].unsqueeze(2).broadcast_to([P, NT, E, E])
            own = pr[:, :, :].unsqueeze(3).broadcast_to([P, NT, E, E])
            lower = tie.rearrange("p (e j) -> p e j", e=E).unsqueeze(1).broadcast_to([P, NT, E, E])
            nc.vector.tensor_tensor(cge[:, :, :, :], other, own, ALU.is_ge)
            link(nc.vector.tensor_tensor(cgt[:, :, :, :], other, own, ALU.is_gt))
            link(nc.vector.tensor_tensor(cge[:, :, :, :], cge[:, :, :, :], lower, ALU.mult))
            link(nc.vector.tensor_tensor(cgt[:, :, :, :], cgt[:, :, :, :], cge[:, :, :, :], ALU.max))
            link(nc.vector.tensor_reduce(rank[:, :, :], cgt[:, :, :, :], AX.X, ALU.add))
            link(nc.vector.scalar_tensor_tensor(gw[:, :, :], rank[:, :, :], 1.5, pr[:, :, :], ALU.is_lt, ALU.mult))
            for last in range(2):
                link(nc.vector.tensor_reduce(col[:, :], gw[:, :, :], AX.X, ALU.add))
                link(nc.vector.tensor_scalar(col[:, :], col[:, :], EPS, None, ALU.add))
                link(nc.vector.reciprocal(rcol[:, :], col[:, :]))
                if not last:
                    link(nc.vector.tensor_tensor(gw[:, :, :], gw[:, :, :], over(rcol[:, :]), ALU.mult))
            nc.vector.scalar_tensor_tensor(gte[:, :, :].rearrange("p e t -> p t e"), gw[:, :, :], 0.5,
                                           over(rcol[:, :]), ALU.mult, ALU.mult).then_inc(F.g, 1)
            dve.wait_ge(F.gT, 1)
            nc.vector.tensor_copy(gT[:, :], bank(4)[:, 0:P]).then_inc(F.gTs, 1)
            nc.vector.memset(mark[:, 0 + 4 * F.f:1 + 4 * F.f], 0.0).then_inc(F.scaled, S0)
            nc.vector.memset(mark[:, 1 + 4 * F.f:2 + 4 * F.f], 0.0).then_inc(F.acc, A0)
            nc.vector.memset(mark[:, 2 + 4 * F.f:3 + 4 * F.f], 0.0).then_inc(F.y, Y0)
            nc.vector.memset(mark[:, 3 + 4 * F.f:4 + 4 * F.f], 0.0).then_inc(F.lo, L0)

            def front(i, s):
                dve.wait_ge(F.y, i * 8 + (s + Y0 - 1))
                for mc in range(MC):
                    dve.wait_ge(F.gelu, i * 32 + (4 * s + mc + 1))
                    nc.vector.tensor_copy(hhi[:, s % 2, mc, :], hf[:, mc, :]).then_inc(F.hi, 1)
                    dve.wait_ge(F.hi, i * 32 + (4 * s + mc + 1))
                    nc.vector.tensor_tensor(hlo[:, s % 2, mc, :], hf[:, mc, :], hhi[:, s % 2, mc, :].bitcast(F32),
                                            ALU.subtract).then_inc(F.lo, 1)

            def back(i, s):
                u, tt = s // GR, s % GR
                if tt == 0:
                    dve.wait_ge(F.gb[u], i * 16 + 16)
                dve.wait_ge(F.y, i * 8 + (s + 1 + Y0))
                dve.wait_ge(F.acc, i * 8 + (s + A0 - 1))
                nc.vector.scalar_tensor_tensor(ysc[:, s % 2, :], bank(4 + s % 2), b2_sb[:, bass.ds(i * 2 + u, 1)],
                                               gb[:, u, tt * 512:(tt + 1) * 512], ALU.add,
                                               ALU.mult).then_inc(F.scaled, 1)
            ffn_units(dve, front, back)

        s_wv = sem("s_wv")
        s_wvhi = sem("s_wvhi")
        s_wvlo = sem("s_wvlo")
        s_v = sem("s_v")
        s_va = sem("s_va")
        s_vd = sem("s_vd")
        s_zero = sem("s_zero")
        s_wq = [sem(f"s_wq{u}") for u in range(2)]
        s_wo = [sem(f"s_wo{u}") for u in range(4)]
        s_wqhi = sem("s_wqhi")
        s_wqs = sem("s_wqs")
        s_proj = sem("s_proj")
        s_cut = sem("s_cut")
        s_k0 = sem("s_k0")
        s_qk = sem("s_qk")
        s_s = sem("s_s")
        s_max = sem("s_max")
        s_exp = sem("s_exp")
        s_hia = sem("s_hia")
        s_hid = sem("s_hid")
        s_lop = sem("s_lop")
        s_lod = sem("s_lod")
        s_rs = sem("s_rs")
        s_vshi = sem("s_vshi")
        s_vs = sem("s_vs")
        s_av = sem("s_av")
        s_o = sem("s_o")
        s_op = sem("s_op")
        s_a = sem("s_a")

        EXP0, AV0, LOP0, LOD0, O0, OP0 = 2, RING, 3, 1, 1, 1
        STEPS = 4 * MT
        WINDOW = 3

        def step(i, b, s):
            return i * STEPS + (b * QUADS * STEPS + s)

        def nth(i, b, s):
            k, r = divmod(s, 4)
            if r < WINDOW:
                return i * (STEPS * 3 // 4) + (b * QUADS * STEPS * 3 // 4 + k * 3 + r)
            return i * (STEPS // 4) + (b * QUADS * STEPS // 4 + k)

        def quads(eng, b, body):
            with eng.Fori(0, QUADS - 1) as i:
                body(i, b, False)
            body(QUADS - 1, b, b == B - 1)

        def pair(i, b, p):
            return i * 2 + (b * PAIRS + p)

        def head(i, b, h):
            return i * 4 + (b * H + h)

        def att_sync(sp):
            sp.wait_ge(norms[1].res, GR)
            sp.wait_ge(ffns[0].scaled, S0 + GR * E)
            sp.dma_start(wvraw[:, :], wv).then_inc(s_wv, 16)

            def load_pair(p, u):
                sp.dma_start(wqraw[:, u, :], wqk[bass.ds(p, 1), :, :].rearrange("a p n -> (a p) n")).then_inc(s_wq[u], 16)

            def load_wo(h, u):
                for part in range(2):
                    sp.dma_start(wo_sb[part * VD:(part + 1) * VD, u, :],
                                 wo[bass.ds(h, 1), :, :].rearrange("a v d -> (a v) d")).then_inc(s_wo[u], 16)

            for p in range(2):
                load_pair(p, p)
            for h in range(4):
                load_wo(h, h)

            def body(i, b, last):
                wrapped = isinstance(i, int)
                if wrapped and last:
                    return
                for u in range(2):
                    sp.wait_ge(s_wqs, pair(i, b, u + 1))
                    load_pair(u if wrapped else i * 2 + (u + 2), u)
                for h in range(4):
                    sp.wait_ge(s_op, head(i, b, h + 1 + OP0))
                    load_wo(h if wrapped else i * 4 + (h + 4), h)
            for b in range(B):
                quads(sp, b, body)

        def att_pe(pe):
            pe.wait_ge(s_wvlo, 1)
            pe.wait_ge(norms[1].lo, GR)
            for unit in range(2 * NT):
                t, half = divmod(unit, 2)
                if unit >= 4:
                    pe.wait_ge((s_va, s_vd)[unit % 2], (unit - 4) // 2 + 1)
                w = slice(half * 512, (half + 1) * 512)
                cols = slice(t * P, (t + 1) * P)
                nc.tensor.matmul(bank(unit % 4), xlo[:, cols], wvhi[:, w], start=True, stop=False)
                nc.tensor.matmul(bank(unit % 4), xhi[:, cols], wvlo[:, w], start=False, stop=False)
                nc.tensor.matmul(bank(unit % 4), xhi[:, cols], wvhi[:, w], start=False, stop=True).then_inc(s_v, 1)
            pe.wait_ge(s_va, NT)
            pe.wait_ge(s_vd, NT)

            def project(i, b, p, what, slot):
                if what == 0:
                    pe.wait_ge(s_wqs, pair(i, b, p + 1))
                w = slice(what * P, (what + 1) * P)
                for half in range(2):
                    cols = slice(b * N + half * 512, b * N + (half + 1) * 512)
                    o = bank(2 * slot + half)
                    u = p % 2
                    nc.tensor.matmul(o, wqlo[:, u, w], xhi[:, cols], start=True, stop=False)
                    nc.tensor.matmul(o, wqhi[:, u, w], xlo[:, cols], start=False, stop=False)
                    last = nc.tensor.matmul(o, wqhi[:, u, w], xhi[:, cols], start=False, stop=True)
                last.then_inc(s_proj, 1)

            def scores(i, b, s, final):
                p, r = divmod(s, 2 * MT)
                hh, m = divmod(r, MT)
                if r == 0:
                    pe.wait_ge(s_qk, pair(i, b, p) * 2 + 2)
                if r in (7, 12) and final and p == 1:
                    pe.wait_ge(s_exp, step(i, b, s + EXP0 - 2))
                elif r in (7, 12):
                    pe.wait_ge(s_qk, pair(i, b, p) * 2 + (3 if r == 7 else 4))
                else:
                    pe.wait_ge(s_exp, step(i, b, s + EXP0 - 1) if slots_back(r) == 2 else step(i, b, s + EXP0))
                slot = ring_slot(r)
                for half in range(2):
                    last = nc.tensor.matmul(bank(2 * slot + half), ks[:, p % 2, hh, m * P:(m + 1) * P],
                                            qs[:, p % 2, half * 512:(half + 1) * 512], start=True, stop=True)
                last.then_inc(s_s, 1)

            def followed(i, b, s, final):
                p, r = divmod(s, 2 * MT)
                if r in (5, 10) and not (final and s >= 2 * MT):
                    pe.wait_ge(s_exp, step(i, b, s - 1 + 1 + EXP0))
                    nb = b
                    ni, np_ = i, p + 1
                    if isinstance(i, int) and i == QUADS - 1 and p == 1:
                        nb, ni, np_ = b + 1, 0, 0
                    project(ni, nb, np_, 0 if r == 5 else 1, 1 - ring_slot(r))

            def products(i, b, s):
                r = s % MT
                k = s % 4
                if k < WINDOW:
                    pe.wait_ge(s_lop, nth(i, b, s) + (1 + LOP0))
                else:
                    pe.wait_ge(s_lod, nth(i, b, s) + (1 + LOD0))
                pe.wait_ge(s_vs, step(i, b, s + 1))
                if r == 0:
                    pe.wait_ge(s_o, head(i, b, s // MT + O0))
                for half in range(2):
                    cols = slice(half * 512, (half + 1) * 512)
                    nc.tensor.matmul(bank(4 + half), vs[:, s % RING, :], elo[:, s % RING, cols],
                                     start=(r == 0), stop=False)
                    last = nc.tensor.matmul(bank(4 + half), vs[:, s % RING, :], ehi[:, s % RING, cols],
                                            start=False, stop=(r == MT - 1))
                last.then_inc(s_av, 1)

            def outproj(i, b, h):
                pe.wait_ge(s_o, head(i, b, h + 1 + O0))
                pe.wait_ge(s_wo[h], i * 32 + (b * QUADS + 1) * 32)
                for half in range(2):
                    last = nc.tensor.matmul(bank(6 + half), wo_sb[:, h, :], oT[:, half * 512:(half + 1) * 512],
                                            start=False, stop=False, skip_group_check=True)
                last.then_inc(s_op, 1)

            def clear_sum():
                for half in range(2):
                    nc.tensor.matmul(bank(6 + half), zero[:, 0:P], zero[:, :], start=True, stop=True,
                                     skip_group_check=True)

            def ahead(i, b, s, final):
                if s >= STEPS and isinstance(i, int) and i == QUADS - 1:
                    i, b, s = 0, b + 1, s - STEPS
                    if b == B:
                        return
                final = final and b == B - 1 and isinstance(i, int) and i == QUADS - 1
                scores(i, b, s, final)
                followed(i, b, s, final)

            pe.wait_ge(s_zero, 1)
            clear_sum()
            project(0, 0, 0, 0, 0)
            project(0, 0, 0, 1, 1)
            for s in range(5):
                ahead(0, 0, s, False)

            def body(i, b, last):
                for s in range(STEPS):
                    if s % MT != 0:
                        ahead(i, b, s + 4, last)
                    products(i, b, s)
                    if s % MT == MT - 1:
                        ahead(i, b, s + 5, last)
                        outproj(i, b, s // MT)
            for b in range(B):
                quads(pe, b, body)
                if b == 0:
                    pe.wait_ge(s_a, 1)
                    clear_sum()

        def ring_slot(r):
            return (r + (r > 5) + (r > 10)) % 2

        def slots_back(r):
            return 1 if r in (6, 11) else 2

        def att_act(act):
            act.wait_ge(s_wv, 16)
            nc.scalar.activation(wvhi[:, :], wvraw[:, :], ACT.Copy).then_inc(s_wvhi, 1)
            for unit in range(0, 2 * NT, 2):
                act.wait_ge(s_v, unit + 1)
                nc.scalar.activation(V[:, unit // 2, 0:512], bank(unit % 4), ACT.Copy).then_inc(s_va, 1)
            nc.scalar.activation(mark[:, 12:13], ident[:, 0:1], ACT.Copy).then_inc(s_exp, EXP0)
            nc.scalar.activation(mark[:, 13:14], ident[:, 0:1], ACT.Copy).then_inc(s_o, O0)

            def cut_high(n, what, slot):
                act.wait_ge(s_proj, n * 2 + (what + 1))
                if not (isinstance(n, int) and n == 0 and what == 0):
                    act.wait_ge(s_qk, n * 2 + what)
                nc.scalar.activation(cut[:, :], bank(2 * slot, 2), ACT.Copy,
                                     scale=(qmask, kmask)[what]).then_inc(s_cut, 1)

            def exps(i, b, s, final):
                if s >= STEPS and isinstance(i, int) and i == QUADS - 1:
                    i, b, s = 0, b + 1, s - STEPS
                    if b == B:
                        return
                p, r = divmod(s, 2 * MT)
                slot = ring_slot(r)
                act.wait_ge(s_max, step(i, b, s + 1))
                if s % 4 < WINDOW:
                    act.wait_ge(s_lop, nth(i, b, s) + (LOP0 - 2))
                else:
                    act.wait_ge(s_lod, nth(i, b, s) + LOD0)
                e = ef[:, s % RING, :]
                nc.scalar.activation(e, bank(2 * slot, 2), ACT.Exp, bias=nmax[:, s % 8:s % 8 + 1],
                                     accum_out=esum[:, s % 8:s % 8 + 1]).then_inc(s_exp, 1)
                if s % 4 < WINDOW:
                    act.wait_ge(s_exp, step(i, b, s + 1 + EXP0))
                    act.wait_ge(s_av, step(i, b, s + AV0 - 3))
                    nc.scalar.activation(ehi[:, s % RING, :], e, ACT.Copy).then_inc(s_hia, 1)
                if r in (5, 10) and not (final and b == B - 1 and isinstance(i, int) and i == QUADS - 1 and p == 1):
                    cut_high(pair(i, b, p + 1), 0 if r == 5 else 1, 1 - slot)

            cut_high(0, 0, 0)
            cut_high(0, 1, 1)
            for s in range(4):
                exps(0, 0, s, False)

            def body(i, b, last):
                for s in range(STEPS):
                    exps(i, b, s + 4, last)
                    if s % MT == MT - 1:
                        h = s // MT
                        act.wait_ge(s_av, step(i, b, s + 1 + AV0))
                        act.wait_ge(s_op, head(i, b, h + OP0))
                        nc.scalar.activation(oT[:, :], bank(4, 2), ACT.Copy).then_inc(s_o, 1)
            for b in range(B):
                quads(act, b, body)
                act.wait_ge(s_op, (b + 1) * H + OP0)
                nc.scalar.activation(aT[:, b * N:(b + 1) * N], bank(6, 2), ACT.Copy).then_inc(s_a, 1)

        def att_dve(dve):
            for unit in range(1, 2 * NT, 2):
                dve.wait_ge(s_v, unit + 1)
                nc.vector.tensor_copy(V[:, unit // 2, 512:1024], bank(unit % 4)).then_inc(s_vd, 1)
            nc.vector.memset(mark[:, 8:9], 0.0).then_inc(s_av, AV0)
            nc.vector.memset(mark[:, 9:10], 0.0).then_inc(s_lop, LOP0)
            nc.vector.memset(mark[:, 10:11], 0.0).then_inc(s_lod, LOD0)
            nc.vector.memset(mark[:, 11:12], 0.0).then_inc(s_op, OP0)
            nc.vector.memset(ks[:, :, :, :].bitcast(F32), 0.0).then_inc(s_k0, 1)
            dve.wait_ge(s_k0, 1)
            dve.wait_ge(s_va, NT)

            def stack(n, u, what, slot):
                dve.wait_ge(s_cut, n * 2 + (what + 1))
                src = bank(2 * slot, 2)
                if what == 0:
                    nc.vector.scalar_tensor_tensor(qs[:, u, :], src, SCALE, cut[:, :].bitcast(F32), ALU.mult,
                                                   ALU.subtract).then_inc(s_qk, 1)
                else:
                    for hh in range(2):
                        rows = slice(hh * 64, (hh + 1) * 64)
                        last = nc.vector.tensor_tensor(ks[rows, u, hh, :], src[rows, :], cut[rows, :].bitcast(F32),
                                                       ALU.subtract)
                    last.then_inc(s_qk, 1)

            def maxima(i, b, s, final):
                if s >= STEPS and isinstance(i, int) and i == QUADS - 1:
                    i, b, s = 0, b + 1, s - STEPS
                    if b == B:
                        return
                p, r = divmod(s, 2 * MT)
                dve.wait_ge(s_s, step(i, b, s + 1))
                nc.vector.tensor_reduce(nmax[:, s % 8:s % 8 + 1], bank(2 * ring_slot(r), 2), AX.X, ALU.max,
                                        negate=True).then_inc(s_max, 1)
                if r in (6, 11) and not (final and b == B - 1 and isinstance(i, int) and i == QUADS - 1 and p == 1):
                    stack(pair(i, b, p + 1), (p + 1) % 2, 0 if r == 6 else 1, 1 - ring_slot(r))

            stack(0, 0, 0, 0)
            stack(0, 0, 1, 1)
            maxima(0, 0, 0, False)

            def body(i, b, last):
                for s in range(STEPS):
                    maxima(i, b, s + 1, last)
                    c = s % 8
                    dve.wait_ge(s_exp, step(i, b, s + 1 + EXP0))
                    nc.vector.reciprocal(rsum[:, c:c + 1], esum[:, c:c + 1]).then_inc(s_rs, 1)
                    dve.wait_ge(s_av, step(i, b, s + AV0 - 3))
                    dve.wait_ge(s_rs, step(i, b, s + 1))
                    v = V[:, b * MT + s % MT, bass.ds(i * 256 + s // MT * VD, VD)]
                    hi, lo = vs[:, s % RING, 0:VD], vs[:, s % RING, VD:2 * VD]
                    nc.vector.tensor_scalar(hi, v, rsum[:, c:c + 1], None, ALU.mult).then_inc(s_vshi, 1)
                    if s % 4 >= WINDOW:
                        nc.vector.tensor_copy(ehi[:, s % RING, :], ef[:, s % RING, :]).then_inc(s_hid, 1)
                    dve.wait_ge(s_vshi, step(i, b, s + 1))
                    nc.vector.scalar_tensor_tensor(lo, v, rsum[:, c:c + 1], hi.bitcast(F32), ALU.mult,
                                                   ALU.subtract).then_inc(s_vs, 1)
                    if s % 4 >= WINDOW:
                        dve.wait_ge(s_hid, nth(i, b, s) + 1)
                        nc.vector.tensor_tensor(elo[:, s % RING, :], ef[:, s % RING, :],
                                                ehi[:, s % RING, :].bitcast(F32), ALU.subtract).then_inc(s_lod, 1)
            for b in range(B):
                quads(dve, b, body)

        def att_pool(pool):
            pool.wait_ge(s_wvhi, 1)
            nc.gpsimd.tensor_tensor(wvlo[:, :], wvraw[:, :], wvhi[:, :].bitcast(F32), ALU.subtract).then_inc(s_wvlo, 1)
            nc.gpsimd.memset(zero[:, :].bitcast(F32), 0.0).then_inc(s_zero, 1)

            def weights(n, u, loads):
                pool.wait_ge(s_wq[u], loads * 16)
                nc.gpsimd.tensor_tensor(wqhi[:, u, :], wqraw[:, u, :], zero[:, 0:2 * P].bitcast(F32),
                                        ALU.add).then_inc(s_wqhi, 1)
                pool.wait_ge(s_wqhi, n + 1)
                nc.gpsimd.tensor_tensor(wqlo[:, u, :], wqraw[:, u, :], wqhi[:, u, :].bitcast(F32),
                                        ALU.subtract).then_inc(s_wqs, 1)
            pool.wait_ge(s_zero, 1)
            weights(0, 0, 1)
            weights(1, 1, 1)

            def body(i, b, last):
                for s in range(STEPS):
                    if s % 4 < WINDOW:
                        pool.wait_ge(s_hia, nth(i, b, s) + 1)
                        pool.wait_ge(s_av, step(i, b, s + AV0 - 3))
                        nc.gpsimd.tensor_tensor(elo[:, s % RING, :], ef[:, s % RING, :],
                                                ehi[:, s % RING, :].bitcast(F32), ALU.subtract).then_inc(s_lop, 1)
                    p, r = divmod(s, 2 * MT)
                    if r == 7 and not last:
                        pool.wait_ge(s_proj, pair(i, b, p) * 2 + 2)
                        weights(pair(i, b, p + 2), p, i + (b * QUADS + 2))
            for b in range(B):
                quads(pool, b, body)

        block = ctx.enter_context(nc.Block())

        @block.sync
        def _(sp):
            sp.dma_start(xt[:, 0:TPG, :], x_v[0]).then_inc(s_x[0], 16)
            sp.dma_start(consts[:, :], cst).then_inc(s_cst, 16)
            for g in range(1, GR):
                sp.dma_start(xt[:, g * TPG:(g + 1) * TPG, :], x_v[g]).then_inc(s_x[g], 16)
            sp.dma_start(wr_sb[:, :], wr).then_inc(s_cst, 16)
            sp.dma_start(br_sb[:, :], br.unsqueeze(0).broadcast_to([P, E])).then_inc(s_cst, 16)
            sp.dma_start(b2_sb[:, :], b2).then_inc(s_cst, 16)
            ffn_sync(sp, ffns[0])
            att_sync(sp)
            sp.wait_ge(s_a, B)
            sp.wait_ge(norms[2].res, GR)
            ffn_sync(sp, ffns[1])
            for g in range(GR):
                sp.wait_ge(norms[3].res, g + 1)
                sp.dma_start(out_v[g], xt[:, g * TPG:(g + 1) * TPG, :]).then_inc(s_out, 16)
            sp.wait_ge(s_out, 16 * GR)
            for F in ffns:
                sp.wait_ge(F.gd, 16)

        @block.gpsimd
        def _(pool):
            nc.gpsimd.memset(mhalf[:, :], -0.5).then_inc(s_fill, 1)
            pool.wait_ge(s_fill, 1)
            norm_pool(pool, norms[0])
            ffn_pool(pool, ffns[0])
            norm_pool(pool, norms[1])
            att_pool(pool)
            norm_pool(pool, norms[2])
            ffn_pool(pool, ffns[1])

        @block.scalar
        def _(act):
            act.wait_ge(s_cst, 64)
            norm_act(act, norms[0])
            ffn_act(act, ffns[0])
            norm_act(act, norms[1])
            att_act(act)
            norm_act(act, norms[2])
            ffn_act(act, ffns[1])

        @block.vector
        def _(dve):
            dve.wait_ge(s_cst, 64)
            norm_dve(dve, norms[0])
            ffn_dve(dve, ffns[0])
            norm_dve(dve, norms[1])
            att_dve(dve)
            norm_dve(dve, norms[2])
            ffn_dve(dve, ffns[1])
            for g in range(GR):
                residual_dve(dve, norms[3], g)

        @block.tensor
        def _(pe):
            pe.wait_ge(s_cst, 64)
            norm_pe(pe, norms[0])
            ffn_pe(pe, ffns[0])
            pe.wait_ge(ffns[0].acc, A0 + GR * E)
            norm_pe(pe, norms[1])
            att_pe(pe)
            pe.wait_ge(s_a, B)
            norm_pe(pe, norms[2])
            ffn_pe(pe, ffns[1])
            pe.wait_ge(ffns[1].acc, A0 + GR * E)
            for g in range(GR):
                back_pe(pe, norms[3], g)


def kernel(L0_attn_x, L0_attn_query_proj, L0_attn_key_proj, L0_attn_value_proj, L0_attn_output_proj,
           L0_ffn_Wr, L0_ffn_br, L0_ffn_W1, L0_ffn_b1, L0_ffn_W2, L0_ffn_b2):
    import numpy as np
    import concourse.bacc as bacc
    from concourse.bass_utils import run_bass_kernel_spmd

    def stacked(heads):
        a = heads.reshape(PAIRS, 2, 1, KD, D)
        a = np.concatenate([a] * PARTS, axis=2)
        return a.reshape(PAIRS, 2 * PARTS * KD, D).transpose(0, 2, 1)

    query = np.asarray(L0_attn_query_proj).reshape(KD, H, D).transpose(1, 0, 2)
    key = np.asarray(L0_attn_key_proj)
    consts = np.zeros((P, C_W), np.float32)
    consts[:, C_ID:C_ID + P] = np.eye(P)
    row = np.arange(P) // KD % PARTS
    consts[:, C_QM] = SCALE * (row >= 2)
    consts[:, C_KM] = row % 2
    consts[:, C_TIE:] = np.tril(np.ones((E, E)), -1).reshape(-1)

    arrays = {
        "x": L0_attn_x,
        "cst": consts,
        "wqk": np.concatenate([stacked(query), stacked(key)], axis=2),
        "wv": np.asarray(L0_attn_value_proj).reshape(H * VD, D).T,
        "wo": np.asarray(L0_attn_output_proj).transpose(1, 2, 0),
        "wr": L0_ffn_Wr,
        "br": L0_ffn_br,
        "w1": L0_ffn_W1,
        "b1": np.asarray(L0_ffn_b1).reshape(E, MC, P).transpose(0, 2, 1),
        "w2": np.asarray(L0_ffn_W2).reshape(E, MC, P, D).transpose(0, 2, 1, 3).reshape(E, P, MC * D),
        "b2": np.asarray(L0_ffn_b2).T,
    }
    nc = bacc.Bacc("TRN2", target_bir_lowering=False, num_devices=1)
    feed, args = {}, []
    for name, a in arrays.items():
        a = np.ascontiguousarray(a)
        feed[f"in_{name}"] = a
        args.append(nc.dram_tensor(f"in_{name}", a.shape, F32, kind="ExternalInput").ap())
    args.append(nc.dram_tensor("out_0", (B, N, D), F32, kind="ExternalOutput").ap())
    macaron_kernel(nc, *args)
    return run_bass_kernel_spmd(nc, [feed], core_ids=[0]).results[0]["out_0"]
```

```python
import concourse.bass as bass
from concourse import mybir
from contextlib import ExitStack

F32 = mybir.dt.float32
F32R = mybir.dt.float32r
ALU = mybir.AluOpType
ACT = mybir.ActivationFunctionType
AX = mybir.AxisListType

P = 128
D = 128
B, N = 2, 1024
TOK = B * N
NT = TOK // P
GR = TOK // 512
TPG = NT // GR
E, M = 8, 512
MC = M // P
H, KD, VD = 16, 16, 64
PAIRS = H // 2
QUADS = H // 4
MT = N // P
LN_EPS = 1e-5
EPS = 1e-9
SCALE = float(KD) ** -0.5
PARTS = 4

C_ID, C_TIE = 0, P
C_W = P + E * E


def macaron_kernel(nc, x, cst, wqk, wv, wo, wr, br, w1, b1, w2, b2, out):
    ctx = ExitStack()
    with ctx:
        def sem(name):
            return ctx.enter_context(nc.semaphore(name))

        def sb(name, shape, dt, stack=ctx):
            return stack.enter_context(nc.sbuf_tensor(name, shape, dt))

        ps = ctx.enter_context(nc.psum_tensor("ps", [P, 8 * 512], F32))

        def bank(b, n=1):
            return ps[:, b * 512:(b + n) * 512]

        xt = sb("xt", [P, NT, D], F32)
        xhi = sb("xhi", [P, TOK], F32R)
        xlo = sb("xlo", [P, TOK], F32R)
        xn = sb("xn", [P, 2, TPG, D], F32)
        consts = sb("consts", [P, C_W], F32)
        ident = consts[:, C_ID:C_ID + P]
        tie = consts[:, C_TIE:C_TIE + E * E]
        stats = sb("stats", [P, NT, 6], F32)
        mv = sb("mv", [P, NT, 2], F32)
        rstd = sb("rstd", [P, NT], F32)
        mark = sb("mark", [P, 14], F32)
        mhalf = sb("mhalf", [P, TPG], F32)
        wr_sb = sb("wr_sb", [P, E], F32)
        br_sb = sb("br_sb", [P, E], F32)
        b1_sb = sb("b1_sb", [P, 2, MC], F32)
        b2_sb = sb("b2_sb", [P, E], F32)

        ffn = ExitStack()
        xf = sb("xf", [P, TOK], F32, ffn)
        acc = sb("acc", [P, TOK], F32, ffn)
        w1raw = sb("w1raw", [P, 2, M], F32, ffn)
        w2raw = sb("w2raw", [P, 2, MC * D], F32, ffn)
        w1hi = sb("w1hi", [P, 2, M], F32R, ffn)
        w1lo = sb("w1lo", [P, 2, M], F32R, ffn)
        w2hi = sb("w2hi", [P, 2, MC * D], F32R, ffn)
        w2lo = sb("w2lo", [P, 2, MC * D], F32R, ffn)
        gb = sb("gb", [P, 2, TOK], F32, ffn)
        hf = sb("hf", [P, MC, 512], F32, ffn)
        hhi = sb("hhi", [P, 2, MC, 512], F32R, ffn)
        hlo = sb("hlo", [P, 2, MC, 512], F32R, ffn)
        ysc = sb("ysc", [P, 2, 512], F32, ffn)
        pr = sb("pr", [P, NT, E], F32, ffn)
        gw = sb("gw", [P, NT, E], F32, ffn)
        rank = sb("rank", [P, NT, E], F32, ffn)
        col = sb("col", [P, NT], F32, ffn)
        rcol = sb("rcol", [P, NT], F32, ffn)
        gte = sb("gte", [P, E, NT], F32, ffn)
        gT = sb("gT", [P, P], F32, ffn)
        cge = sb("cge", [P, NT, E, E], F32, ffn)
        cgt = sb("cgt", [P, NT, E, E], F32, ffn)
        ffn.close()

        att = ExitStack()
        V = sb("V", [P, NT, H * VD], F32, att)
        early = ExitStack()
        wqkraw = sb("wqkraw", [P, 4 * P], F32, early)
        wqkhi = sb("wqkhi", [P, 4 * P], F32R, early)
        wqklo = sb("wqklo", [P, 4 * P], F32R, early)
        wvraw = sb("wvraw", [P, H * VD], F32, early)
        wvhi = sb("wvhi", [P, H * VD], F32R, early)
        wvlo = sb("wvlo", [P, H * VD], F32R, early)
        sthi = sb("sthi", [P, 4, 512], F32R, early)
        stlo = sb("stlo", [P, 4, 512], F32R, early)
        early.close()
        RING = 4
        ef = sb("ef", [P, RING, N], F32, att)
        ehi = sb("ehi", [P, RING, N], F32R, att)
        elo = sb("elo", [P, RING, N], F32R, att)
        efn = sb("efn", [P, 2, N], F32, att)
        qs = sb("qs", [P, 2, N], F32R, att)
        ks = sb("ks", [P, 2, 2, N], F32R, att)
        vs = sb("vs", [P, RING, 2 * VD], F32R, att)
        vsn = sb("vsn", [P, 2, VD], F32, att)
        oT = sb("oT", [P, 2, N], F32, att)
        wo_sb = sb("wo_sb", [P, 4, D], F32, att)
        nmax = sb("nmax", [P, 8], F32, att)
        esum = sb("esum", [P, 8], F32, att)
        rsum = sb("rsum", [P, 8], F32, att)
        aT = sb("aT", [P, TOK], F32, att)
        att.close()

        qkd = nc.dram_tensor("qk_parts", [2, 2, H, KD, TOK], F32, kind="Internal").ap()
        gd = [nc.dram_tensor(f"gates{f}", [P, P], F32, kind="Internal").ap() for f in range(2)]

        x_v = x.rearrange("b n d -> (b n) d").rearrange("(g t p) d -> g p t d", g=GR, p=P)
        out_v = out.rearrange("b n d -> (b n) d").rearrange("(g t p) d -> g p t d", g=GR, p=P)

        s_x = [sem(f"s_x{g}") for g in range(GR)]
        s_cst = sem("s_cst")
        s_fill = sem("s_fill")
        s_out = sem("s_out")

        class Norm:
            def __init__(self, k, src):
                self.k, self.src = k, src
                self.back = sem(f"n{k}_back")
                self.res = sem(f"n{k}_res")
                self.st = sem(f"n{k}_st")
                self.mv = sem(f"n{k}_mv")
                self.eps = sem(f"n{k}_eps")
                self.rstd = sem(f"n{k}_rstd")
                self.xn = sem(f"n{k}_xn")
                self.fwd = sem(f"n{k}_fwd")
                self.x32 = sem(f"n{k}_x32")
                self.hi = sem(f"n{k}_hi")
                self.lo = sem(f"n{k}_lo")

        norms = [Norm(0, None), Norm(1, acc), Norm(2, aT), Norm(3, acc)]

        def back_pe(pe, n, g):
            if g >= 2:
                pe.wait_ge(n.res, g - 1)
            for t in range(TPG):
                at = (g * TPG + t) * P
                last = nc.tensor.transpose(bank(g % 2)[:, t * P:(t + 1) * P], n.src[:, at:at + P], ident)
            last.then_inc(n.back, 1)

        def residual_dve(dve, n, g):
            dve.wait_ge(n.back, g + 1)
            xg = xt[:, g * TPG:(g + 1) * TPG, :]
            nc.vector.tensor_tensor(xg, xg, bank(g % 2).rearrange("p (t d) -> p t d", d=D), ALU.add).then_inc(n.res, 1)

        def norm_pe(pe, n):
            if n.src is not None:
                for g in range(GR):
                    back_pe(pe, n, g)
            for g in range(GR):
                pe.wait_ge(n.xn, g + 1)
                if g >= 2:
                    pe.wait_ge(n.lo, g - 1)
                for t in range(TPG):
                    last = nc.tensor.transpose(bank(6 + g % 2)[:, t * P:(t + 1) * P], xn[:, g % 2, t, :], ident)
                last.then_inc(n.fwd, 1)

        def norm_act(act, n):
            for g in range(GR):
                cols = slice(g * 512, (g + 1) * 512)
                act.wait_ge(n.fwd, g + 1)
                if n.k != 1:
                    nc.scalar.activation(xf[:, cols], bank(6 + g % 2), ACT.Copy).then_inc(n.x32, 1)
                nc.scalar.activation(xhi[:, cols], bank(6 + g % 2), ACT.Copy).then_inc(n.hi, 1)

        def norm_pool(pool, n):
            for g in range(GR):
                r = rstd[:, g * TPG:(g + 1) * TPG]
                pool.wait_ge(n.mv, g + 1)
                nc.gpsimd.tensor_scalar(r, mv[:, g * TPG:(g + 1) * TPG, 1], LN_EPS, None, ALU.add).then_inc(n.eps, 1)
                pool.wait_ge(n.eps, g + 1)
                nc.gpsimd.tensor_tensor(r, r, mhalf[:, :], ALU.pow).then_inc(n.rstd, 1)

        def norm_dve(dve, n):
            def statistics(g):
                if n.src is None:
                    dve.wait_ge(s_x[g], 16)
                else:
                    residual_dve(dve, n, g)
                    dve.wait_ge(n.res, g + 1)
                for t in range(g * TPG, (g + 1) * TPG):
                    last = nc.vector.bn_stats(stats[:, t, :], xt[:, t, :])
                last.then_inc(n.st, 1)
                dve.wait_ge(n.st, g + 1)
                for t in range(g * TPG, (g + 1) * TPG):
                    last = nc.vector.bn_aggr(mv[:, t, :], stats[:, t, :])
                last.then_inc(n.mv, 1)

            def scaled(g):
                dve.wait_ge(n.rstd, g + 1)
                if g >= 2:
                    dve.wait_ge(n.fwd, g - 1)
                for t in range(TPG):
                    a = g * TPG + t
                    last = nc.vector.tensor_scalar(xn[:, g % 2, t, :], xt[:, a, :], mv[:, a, 0:1], rstd[:, a:a + 1],
                                                   ALU.subtract, ALU.mult)
                last.then_inc(n.xn, 1)

            def low(g):
                cols = slice(g * 512, (g + 1) * 512)
                dve.wait_ge(n.hi, g + 1)
                nc.vector.tensor_tensor(xlo[:, cols], bank(6 + g % 2), xhi[:, cols].bitcast(F32),
                                        ALU.subtract).then_inc(n.lo, 1)

            for g in range(GR + 2):
                if g < GR:
                    statistics(g)
                if 0 <= g - 1 < GR:
                    scaled(g - 1)
                if g >= 2:
                    low(g - 2)

        class Ffn:
            def __init__(self, f, n):
                self.f, self.n = f, n
                self.logit = sem(f"f{f}_logit")
                self.sh = sem(f"f{f}_sh")
                self.ex = sem(f"f{f}_ex")
                self.chain = sem(f"f{f}_chain")
                self.g = sem(f"f{f}_g")
                self.gT = sem(f"f{f}_gT")
                self.gTs = sem(f"f{f}_gTs")
                self.gd = sem(f"f{f}_gd")
                self.acc0 = sem(f"f{f}_acc0")
                self.whi = sem(f"f{f}_whi")
                self.wready = sem(f"f{f}_wready")
                self.h = sem(f"f{f}_h")
                self.gelu = sem(f"f{f}_gelu")
                self.hi = sem(f"f{f}_hi")
                self.lo = sem(f"f{f}_lo")
                self.y = sem(f"f{f}_y")
                self.scaled = sem(f"f{f}_scaled")
                self.acc = sem(f"f{f}_acc")
                self.w = [sem(f"f{f}_w{u}") for u in range(2)]
                self.gb = [sem(f"f{f}_gb{u}") for u in range(2)]
                self.b1 = [sem(f"f{f}_b1{u}") for u in range(2)]

        ffns = [Ffn(0, norms[0]), Ffn(1, norms[2])]

        Y0 = S0 = A0 = 2
        L0 = 4

        def load_expert(q, F, e, u):
            q.dma_start(w1raw[:, u, :], w1[bass.ds(e, 1), :, :].rearrange("a p n -> (a p) n")).then_inc(F.w[u], 16)
            q.dma_start(w2raw[:, u, :], w2[bass.ds(e, 1), :, :].rearrange("a p n -> (a p) n")).then_inc(F.w[u], 16)

        def load_gates(q, F, e, u):
            src = gd[F.f].rearrange("a b -> (a b)").rearrange("(e n) -> e n", e=E)[bass.ds(e, 1), :]
            q.dma_start(gb[:, u, :], src.broadcast_to([P, TOK])).then_inc(F.gb[u], 16)

        def load_bias(q, F, e, u):
            q.dma_start(b1_sb[:, u, :], b1[bass.ds(e, 1), :, :].rearrange("a p n -> (a p) n")).then_inc(F.b1[u], 16)

        def ffn_sync(sp, F):
            for e in range(2):
                load_expert(sp, F, e, e)
                load_bias(sp, F, e, e)
            sp.wait_ge(F.gTs, 1)
            sp.dma_start(gd[F.f], gT[:, :]).then_inc(F.gd, 16)
            sp.wait_ge(F.gd, 16)
            for e in range(2):
                load_gates(sp, F, e, e)
            with sp.Fori(0, E // 2 - 1) as i:
                for u in range(2):
                    sp.wait_ge(F.wready, i * 2 + (u + 1))
                    load_expert(sp, F, i * 2 + (u + 2), u)
                for u in range(2):
                    sp.wait_ge(F.scaled, i * 8 + (S0 + 4 * (u + 1)))
                    load_bias(sp, F, i * 2 + (u + 2), u)
                    load_gates(sp, F, i * 2 + (u + 2), u)

        def ffn_units(eng, front, back):
            def body(i, last):
                for s in range(2 * GR):
                    if not (last and s == 2 * GR - 1):
                        front(i, s + 1)
                    back(i, s)
            front(0, 0)
            with eng.Fori(0, E // 2 - 1) as i:
                body(i, False)
            body(E // 2 - 1, True)

        def next_expert(i, s):
            return s % GR == 1 and not (isinstance(i, int) and i == E // 2 - 1 and s >= GR)

        def ffn_pe(pe, F):
            n = F.n
            for t in range(NT):
                if t % TPG == 0:
                    pe.wait_ge(n.x32, t // TPG + 1)
                last = nc.tensor.matmul(bank(5)[:, t * E:(t + 1) * E], xf[:, t * P:(t + 1) * P], wr_sb[:, :],
                                        start=True, stop=True)
            last.then_inc(F.logit, 1)
            pe.wait_ge(n.lo, GR)

            def hidden(i, s, mc):
                u, tt = (s // GR) % 2, s % GR
                if tt == 0 and mc == 0:
                    pe.wait_ge(F.wready, i * 2 + (s // GR + 1))
                if not (isinstance(i, int) and i == 0 and s == 0):
                    pe.wait_ge(F.gelu, i * 32 + (4 * s + mc - 3))
                w = slice(mc * P, (mc + 1) * P)
                cols = slice(tt * 512, (tt + 1) * 512)
                nc.tensor.matmul(bank(mc), w1lo[:, u, w], xhi[:, cols], start=True, stop=False)
                nc.tensor.matmul(bank(mc), w1hi[:, u, w], xlo[:, cols], start=False, stop=False)
                nc.tensor.matmul(bank(mc), w1hi[:, u, w], xhi[:, cols], start=False, stop=True).then_inc(F.h, 1)

            def output(i, s, mc):
                u, tt = s // GR, s % GR
                if mc == 0:
                    pe.wait_ge(F.scaled, i * 8 + (s + S0 - 1))
                pe.wait_ge(F.lo, i * 32 + (4 * s + mc + 1 + L0))
                w = slice(mc * D, (mc + 1) * D)
                y = bank(4 + s % 2)
                nc.tensor.matmul(y, w2lo[:, u, w], hhi[:, s % 2, mc, :], start=(mc == 0), stop=False)
                nc.tensor.matmul(y, w2hi[:, u, w], hlo[:, s % 2, mc, :], start=False, stop=False)
                last = nc.tensor.matmul(y, w2hi[:, u, w], hhi[:, s % 2, mc, :], start=False, stop=(mc == MC - 1))
                if mc == MC - 1:
                    last.then_inc(F.y, 1)

            for mc in range(MC):
                hidden(0, 0, mc)
            pe.wait_ge(F.g, 1)
            nc.tensor.transpose(bank(4)[:, 0:P], gte[:, :, :].rearrange("p e t -> p (e t)"), ident).then_inc(F.gT, 1)
            pe.wait_ge(F.gTs, 1)

            def body(i, last):
                for s in range(2 * GR):
                    for mc in range(MC):
                        if not (last and s == 2 * GR - 1):
                            hidden(i, s + 1, mc)
                        output(i, s, mc)
            with pe.Fori(0, E // 2 - 1) as i:
                body(i, False)
            body(E // 2 - 1, True)

        def ffn_act(act, F):
            act.wait_ge(F.sh, 1)
            nc.scalar.activation(pr[:, :, :], pr[:, :, :], ACT.Exp).then_inc(F.ex, 1)

            def weights(i, u):
                nc.scalar.activation(w1hi[:, u, :], w1raw[:, u, :], ACT.Copy)
                nc.scalar.activation(w2hi[:, u, :], w2raw[:, u, :], ACT.Copy).then_inc(F.whi, 1)

            act.wait_ge(F.w[0], 32)
            weights(0, 0)

            def front(i, s):
                u = s // GR % 2
                if s % GR == 0:
                    act.wait_ge(F.b1[u], i * 16 + (s // (2 * GR) + 1) * 16)
                for mc in range(MC):
                    act.wait_ge(F.h, i * 32 + (4 * s + mc + 1))
                    act.wait_ge(F.lo, i * 32 + (4 * s + mc + 1))
                    nc.scalar.activation(hf[:, mc, :], bank(mc), ACT.Gelu,
                                         bias=b1_sb[:, u, mc:mc + 1]).then_inc(F.gelu, 1)

            def back(i, s):
                if next_expert(i, s):
                    u = (s // GR + 1) % 2
                    e = i * 2 + s // GR
                    act.wait_ge(F.y, e * 4 + Y0)
                    act.wait_ge(F.w[u], (i + (s // GR + 1) // 2) * 32 + 32)
                    weights(i, u)
            ffn_units(act, front, back)

        def ffn_pool(pool, F):
            nc.gpsimd.memset(acc[:, :], 0.0).then_inc(F.acc0, 1)

            def weights(u):
                nc.gpsimd.tensor_tensor(w1lo[:, u, :], w1raw[:, u, :], w1hi[:, u, :].bitcast(F32), ALU.subtract)
                nc.gpsimd.tensor_tensor(w2lo[:, u, :], w2raw[:, u, :], w2hi[:, u, :].bitcast(F32),
                                        ALU.subtract).then_inc(F.wready, 1)

            pool.wait_ge(F.whi, 1)
            weights(0)
            pool.wait_ge(F.acc0, 1)

            def body(i, last):
                for s in range(2 * GR):
                    tt = s % GR
                    pool.wait_ge(F.scaled, i * 8 + (s + 1 + S0))
                    a = acc[:, tt * 512:(tt + 1) * 512]
                    nc.gpsimd.tensor_tensor(a, a, ysc[:, s % 2, :], ALU.add).then_inc(F.acc, 1)
                    if tt == 0 and next_expert(i, s + 1):
                        pool.wait_ge(F.whi, i * 2 + (s // GR + 2))
                        weights((s // GR + 1) % 2)
            with pool.Fori(0, E // 2 - 1) as i:
                body(i, False)
            body(E // 2 - 1, True)

        def ffn_dve(dve, F):
            count = [0]

            def link(ins):
                count[0] += 1
                ins.then_inc(F.chain, 1)
                dve.wait_ge(F.chain, count[0])

            def over(t):
                return t.unsqueeze(2).broadcast_to([P, NT, E])

            dve.wait_ge(F.logit, 1)
            link(nc.vector.tensor_tensor(pr[:, :, :], bank(5)[:, 0:NT * E].rearrange("p (t e) -> p t e", e=E),
                                         br_sb[:, :].unsqueeze(1).broadcast_to([P, NT, E]), ALU.add))
            link(nc.vector.tensor_reduce(col[:, :], pr[:, :, :], AX.X, ALU.max))
            nc.vector.tensor_tensor(pr[:, :, :], pr[:, :, :], over(col[:, :]), ALU.subtract).then_inc(F.sh, 1)
            dve.wait_ge(F.ex, 1)
            link(nc.vector.tensor_reduce(col[:, :], pr[:, :, :], AX.X, ALU.add))
            link(nc.vector.reciprocal(rcol[:, :], col[:, :]))
            link(nc.vector.tensor_tensor(pr[:, :, :], pr[:, :, :], over(rcol[:, :]), ALU.mult))
            other = pr[:, :, :].unsqueeze(2).broadcast_to([P, NT, E, E])
            own = pr[:, :, :].unsqueeze(3).broadcast_to([P, NT, E, E])
            lower = tie.rearrange("p (e j) -> p e j", e=E).unsqueeze(1).broadcast_to([P, NT, E, E])
            nc.vector.tensor_tensor(cge[:, :, :, :], other, own, ALU.is_ge)
            link(nc.vector.tensor_tensor(cgt[:, :, :, :], other, own, ALU.is_gt))
            link(nc.vector.tensor_tensor(cge[:, :, :, :], cge[:, :, :, :], lower, ALU.mult))
            link(nc.vector.tensor_tensor(cgt[:, :, :, :], cgt[:, :, :, :], cge[:, :, :, :], ALU.max))
            link(nc.vector.tensor_reduce(rank[:, :, :], cgt[:, :, :, :], AX.X, ALU.add))
            link(nc.vector.scalar_tensor_tensor(gw[:, :, :], rank[:, :, :], 1.5, pr[:, :, :], ALU.is_lt, ALU.mult))
            for last in range(2):
                link(nc.vector.tensor_reduce(col[:, :], gw[:, :, :], AX.X, ALU.add))
                link(nc.vector.tensor_scalar(col[:, :], col[:, :], EPS, None, ALU.add))
                link(nc.vector.reciprocal(rcol[:, :], col[:, :]))
                if not last:
                    link(nc.vector.tensor_tensor(gw[:, :, :], gw[:, :, :], over(rcol[:, :]), ALU.mult))
            nc.vector.scalar_tensor_tensor(gte[:, :, :].rearrange("p e t -> p t e"), gw[:, :, :], 0.5,
                                           over(rcol[:, :]), ALU.mult, ALU.mult).then_inc(F.g, 1)
            dve.wait_ge(F.gT, 1)
            nc.vector.tensor_copy(gT[:, :], bank(4)[:, 0:P]).then_inc(F.gTs, 1)
            nc.vector.memset(mark[:, 0 + 4 * F.f:1 + 4 * F.f], 0.0).then_inc(F.scaled, S0)
            nc.vector.memset(mark[:, 1 + 4 * F.f:2 + 4 * F.f], 0.0).then_inc(F.acc, A0)
            nc.vector.memset(mark[:, 2 + 4 * F.f:3 + 4 * F.f], 0.0).then_inc(F.y, Y0)
            nc.vector.memset(mark[:, 3 + 4 * F.f:4 + 4 * F.f], 0.0).then_inc(F.lo, L0)

            def front(i, s):
                dve.wait_ge(F.y, i * 8 + (s + Y0 - 1))
                for mc in range(MC):
                    dve.wait_ge(F.gelu, i * 32 + (4 * s + mc + 1))
                    nc.vector.tensor_copy(hhi[:, s % 2, mc, :], hf[:, mc, :]).then_inc(F.hi, 1)
                    dve.wait_ge(F.hi, i * 32 + (4 * s + mc + 1))
                    nc.vector.tensor_tensor(hlo[:, s % 2, mc, :], hf[:, mc, :], hhi[:, s % 2, mc, :].bitcast(F32),
                                            ALU.subtract).then_inc(F.lo, 1)

            def back(i, s):
                u, tt = s // GR, s % GR
                if tt == 0:
                    dve.wait_ge(F.gb[u], i * 16 + 16)
                dve.wait_ge(F.y, i * 8 + (s + 1 + Y0))
                dve.wait_ge(F.acc, i * 8 + (s + A0 - 1))
                nc.vector.scalar_tensor_tensor(ysc[:, s % 2, :], bank(4 + s % 2), b2_sb[:, bass.ds(i * 2 + u, 1)],
                                               gb[:, u, tt * 512:(tt + 1) * 512], ALU.add,
                                               ALU.mult).then_inc(F.scaled, 1)
            ffn_units(dve, front, back)

        s_wv = sem("s_wv")
        s_wqk = sem("s_wqk")
        s_whi = sem("s_whi")
        s_wlo = sem("s_wlo")
        s_qk = sem("s_qk")
        s_qkhi = sem("s_qkhi")
        s_qklo = sem("s_qklo")
        s_st = [sem(f"s_st{u}") for u in range(4)]
        s_v = sem("s_v")
        s_va = sem("s_va")
        s_vd = sem("s_vd")
        s_k0 = sem("s_k0")
        s_a0 = sem("s_a0")
        s_pair = [sem(f"s_pair{u}") for u in range(2)]
        s_wo = [sem(f"s_wo{u}") for u in range(4)]
        s_s = sem("s_s")
        s_max = sem("s_max")
        s_exp = sem("s_exp")
        s_hi = sem("s_hi")
        s_lo = sem("s_lo")
        s_rs = sem("s_rs")
        s_vsh = sem("s_vsh")
        s_vsl = sem("s_vsl")
        s_vsn = sem("s_vsn")
        s_av = sem("s_av")
        s_avh = sem("s_avh")
        s_o = sem("s_o")
        s_op = sem("s_op")
        s_sum = sem("s_sum")

        EXP0, LO0, AV0, O0, OP0, SUM0 = 3, RING, 8, 2, 2, 1
        STEPS = 4 * MT
        PST = 2 * MT
        WHOLE = 1
        SPLIT = [0, 2, 3]

        def step(i, b, s):
            return i * STEPS + (b * QUADS * STEPS + s)

        def is_whole(s):
            return s % 4 == WHOLE

        def nth(i, b, s):
            k, r = divmod(s, 4)
            if r == WHOLE:
                return i * (STEPS // 4) + (b * QUADS * STEPS // 4 + k)
            return i * (STEPS * 3 // 4) + (b * QUADS * STEPS * 3 // 4 + k * 3 + SPLIT.index(r))

        def slot_of(s):
            return (s // 4 * 3 + SPLIT.index(s % 4)) % RING

        def wait_slot(eng, i, b, s):
            if is_whole(s):
                back = 8
            else:
                back = 6 if s % 4 == 2 else 5
            eng.wait_ge(s_av, step(i, b, s + (AV0 + 1 - back)))

        LEAD = 6

        def turn(r):
            return r - 2 if r < LEAD else r - 1 if r < LEAD + 6 else r

        def ring_slot(s):
            return turn(s % PST) % 3
        OUT_SLOT = (LEAD - 2) % 3

        def steps_back(r):
            return {LEAD: 2, LEAD + 1: 2, LEAD + 6: 2, LEAD + 7: 2, LEAD + 8: 5}.get(r, 3)

        def quads(eng, b, body):
            with eng.Fori(0, QUADS - 1) as i:
                body(i, b)
            body(QUADS - 1, b)

        def placed(i, b, s):
            if s >= STEPS and isinstance(i, int) and i == QUADS - 1:
                i, b, s = 0, b + 1, s - STEPS
            return (i, b, s) if b < B else None

        def pair(i, b, p):
            return i * 2 + (b * PAIRS + p)

        def head(i, b, h):
            return i * 4 + (b * H + h)

        UNITS = [(what, hg, g) for g in range(GR) for what in range(2) for hg in range(2)]

        def att_sync(sp):
            sp.wait_ge(norms[1].res, GR)
            sp.dma_start(wqkraw[:, :], wqk).then_inc(s_wqk, 16)
            sp.dma_start(wvraw[:, :], wv).then_inc(s_wv, 16)

            def load_pair(b, j, u):
                cols = slice(b * N, (b + 1) * N)
                for hh in range(2):
                    for c in range(PARTS):
                        rows = slice(hh * 64 + c * KD, hh * 64 + (c + 1) * KD)
                        for what, dst, part in ((0, qs[rows, u, :], c // 2), (1, ks[rows, u, hh, :], c % 2)):
                            src = qkd[what, part, bass.ds(j * 2 + hh, 1), :, cols]
                            sp.dma_start(dst.bitcast(F32), src.rearrange("a k n -> (a k) n")).then_inc(s_pair[u], 16)

            def load_wo(h, u):
                for part in range(2):
                    sp.dma_start(wo_sb[part * VD:(part + 1) * VD, u, :],
                                 wo[bass.ds(h, 1), :, :].rearrange("a v d -> (a v) d")).then_inc(s_wo[u], 16)

            for n, (what, hg, g) in enumerate(UNITS):
                sp.wait_ge(s_qklo, n + 1)
                rows = slice(hg * 8, hg * 8 + 8)
                for part, st in enumerate((sthi, stlo)):
                    dst = qkd[what, part, rows, :, g * 512:(g + 1) * 512].rearrange("h k n -> (h k) n")
                    sp.dma_start(dst, st[:, n % 4, :].bitcast(F32)).then_inc(s_st[n % 4], 16)
            for u in range(4):
                sp.wait_ge(s_st[u], 32 * len(UNITS) // 4)
            sp.wait_ge(s_k0, 1)
            for p in range(2):
                load_pair(0, p, p)
            for h in range(4):
                load_wo(h, h)

            def body(i, b):
                wrapped = isinstance(i, int)
                if wrapped and b == B - 1:
                    return
                for u in range(2):
                    sp.wait_ge(s_s, step(i, b, (u + 1) * PST))
                    if wrapped:
                        load_pair(b + 1, u, u)
                    else:
                        load_pair(b, i * 2 + (u + 2), u)
                    for h in (2 * u, 2 * u + 1):
                        sp.wait_ge(s_op, head(i, b, h + 1 + OP0))
                        load_wo(h if wrapped else i * 4 + (h + 4), h)
            for b in range(B):
                quads(sp, b, body)

        def att_pe(pe):
            pe.wait_ge(s_wlo, 1)
            for n, (what, hg, g) in enumerate(UNITS):
                if what == 0 and hg == 0:
                    pe.wait_ge(norms[1].lo, g + 1)
                if n >= 4:
                    pe.wait_ge(s_qklo, n - 3)
                cols = slice(g * 512, (g + 1) * 512)
                w = slice((what * 2 + hg) * P, (what * 2 + hg + 1) * P)
                nc.tensor.matmul(bank(n % 4), wqklo[:, w], xhi[:, cols], start=True, stop=False)
                nc.tensor.matmul(bank(n % 4), wqkhi[:, w], xlo[:, cols], start=False, stop=False)
                nc.tensor.matmul(bank(n % 4), wqkhi[:, w], xhi[:, cols], start=False, stop=True).then_inc(s_qk, 1)
            pe.wait_ge(s_wlo, 2)
            for unit in range(2 * NT):
                t, half = divmod(unit, 2)
                if unit >= 4:
                    pe.wait_ge((s_va, s_vd)[unit % 2], (unit - 4) // 2 + 1)
                w = slice(half * 512, (half + 1) * 512)
                cols = slice(t * P, (t + 1) * P)
                o = bank(4 + unit % 4)
                nc.tensor.matmul(o, xlo[:, cols], wvhi[:, w], start=True, stop=False)
                nc.tensor.matmul(o, xhi[:, cols], wvlo[:, w], start=False, stop=False)
                nc.tensor.matmul(o, xhi[:, cols], wvhi[:, w], start=False, stop=True).then_inc(s_v, 1)
            pe.wait_ge(s_va, NT)
            pe.wait_ge(s_vd, NT)

            def scores(i, b, s):
                if placed(i, b, s) is None:
                    return
                i, b, s = placed(i, b, s)
                p, r = divmod(s, PST)
                hh, m = divmod(r, MT)
                if r == 0:
                    pe.wait_ge(s_pair[p % 2], i * (256) + ((b * QUADS + p // 2) * 256 + 256))
                if r == LEAD + 2:
                    pe.wait_ge(s_sum, pair(i, b, p) + SUM0)
                else:
                    pe.wait_ge(s_exp, step(i, b, s + (EXP0 + 1 - steps_back(r))))
                slot = ring_slot(r)
                for half in range(2):
                    last = nc.tensor.matmul(bank(2 * slot + half), ks[:, p % 2, hh, m * P:(m + 1) * P],
                                            qs[:, p % 2, half * 512:(half + 1) * 512], start=True, stop=True)
                last.then_inc(s_s, 1)

            def products(i, b, s):
                r = s % MT
                if is_whole(s):
                    pe.wait_ge(s_exp, step(i, b, s + (1 + EXP0)))
                    pe.wait_ge(s_vsn, nth(i, b, s) + 1)
                else:
                    pe.wait_ge(s_lo, nth(i, b, s) + (1 + LO0))
                    pe.wait_ge(s_vsl, nth(i, b, s) + 1)
                for half in range(2):
                    cols = slice(half * 512, (half + 1) * 512)
                    if r == 0:
                        pe.wait_ge(s_o, head(i, b, s // MT) * 2 + (half + 1))
                    if is_whole(s):
                        n = s // 4 % 2
                        last = nc.tensor.matmul(bank(6 + half)[0:VD, :], vsn[:, n, :], efn[:, n, cols],
                                                start=False, stop=False)
                    else:
                        n = slot_of(s)
                        nc.tensor.matmul(bank(6 + half), vs[:, n, :], elo[:, n, cols], start=(r == 0), stop=False)
                        last = nc.tensor.matmul(bank(6 + half), vs[:, n, :], ehi[:, n, cols],
                                                start=False, stop=(r == MT - 1))
                    if half == 0 and r == MT - 1:
                        last.then_inc(s_avh, 1)
                last.then_inc(s_av, 1)

            def outproj(i, b, h):
                pe.wait_ge(s_o, head(i, b, h) * 2 + (2 + O0))
                pe.wait_ge(s_wo[h], i * 32 + (b * QUADS + 1) * 32)
                for half in range(2):
                    last = nc.tensor.matmul(bank(2 * OUT_SLOT + half), wo_sb[:, h, :],
                                            oT[:, h % 2, half * 512:(half + 1) * 512],
                                            start=(h % 2 == 0), stop=(h % 2 == 1))
                last.then_inc(s_op, 1)

            for s in range(LEAD + 1):
                scores(0, 0, s)

            def body(i, b):
                for s in range(STEPS):
                    r = s % PST
                    if r != 0:
                        scores(i, b, s + LEAD)
                    if r == PST - 1:
                        ahead = LEAD - 2
                        while placed(i, b, s + ahead) is None or ring_slot(s + ahead) != OUT_SLOT:
                            ahead -= 1
                        pe.wait_ge(s_exp, step(i, b, s + ahead + (1 + EXP0)))
                        outproj(i, b, s // MT - 1)
                    products(i, b, s)
                    if r == PST - 1:
                        scores(i, b, s + LEAD + 1)
                        outproj(i, b, s // MT)
            for b in range(B):
                quads(pe, b, body)

        def att_act(act):
            act.wait_ge(s_wqk, 16)
            nc.scalar.activation(wqkhi[:, :], wqkraw[:, :], ACT.Copy).then_inc(s_whi, 1)
            act.wait_ge(s_wv, 16)
            nc.scalar.activation(wvhi[:, :], wvraw[:, :], ACT.Copy).then_inc(s_whi, 1)
            for n, (what, hg, g) in enumerate(UNITS):
                act.wait_ge(s_qk, n + 1)
                if n >= 4:
                    act.wait_ge(s_st[n % 4], 32 * (n // 4))
                nc.scalar.activation(sthi[:, n % 4, :], bank(n % 4), ACT.Copy,
                                     scale=(SCALE, 1.0)[what]).then_inc(s_qkhi, 1)
            for unit in range(0, 2 * NT, 2):
                act.wait_ge(s_v, unit + 1)
                nc.scalar.activation(V[:, unit // 2, 0:512], bank(4 + unit % 4), ACT.Copy).then_inc(s_va, 1)
            nc.scalar.activation(mark[:, 12:13], ident[:, 0:1], ACT.Copy).then_inc(s_exp, EXP0)

            def exps(i, b, s):
                at = placed(i, b, s)
                if at:
                    i1, b1, s1 = at
                    c = s1 % 8
                    act.wait_ge(s_max, step(i1, b1, s1 + 1))
                    if is_whole(s1):
                        wait_slot(act, i1, b1, s1)
                        e = efn[:, s1 // 4 % 2, :]
                    else:
                        act.wait_ge(s_lo, nth(i1, b1, s1) + 1)
                        e = ef[:, slot_of(s1), :]
                    nc.scalar.activation(e, bank(2 * ring_slot(s1), 2), ACT.Exp, bias=nmax[:, c:c + 1],
                                         accum_out=esum[:, c:c + 1]).then_inc(s_exp, 1)
                if s > 0 and not is_whole(s - 1):
                    i1, b1, s1 = placed(i, b, s - 1)
                    act.wait_ge(s_exp, step(i1, b1, s1 + (1 + EXP0)))
                    wait_slot(act, i1, b1, s1)
                    n = slot_of(s1)
                    nc.scalar.activation(ehi[:, n, :], ef[:, n, :], ACT.Copy).then_inc(s_hi, 1)

            exps(0, 0, 0)

            def body(i, b):
                for s in range(STEPS):
                    exps(i, b, s + 1)
            for b in range(B):
                quads(act, b, body)

        def att_dve(dve):
            for n, (what, hg, g) in enumerate(UNITS):
                dve.wait_ge(s_qkhi, n + 1)
                nc.vector.scalar_tensor_tensor(stlo[:, n % 4, :], bank(n % 4), (SCALE, 1.0)[what],
                                               sthi[:, n % 4, :].bitcast(F32), ALU.mult,
                                               ALU.subtract).then_inc(s_qklo, 1)
            for unit in range(1, 2 * NT, 2):
                dve.wait_ge(s_v, unit + 1)
                nc.vector.tensor_copy(V[:, unit // 2, 512:1024], bank(4 + unit % 4)).then_inc(s_vd, 1)
            nc.vector.memset(mark[:, 8:9], 0.0).then_inc(s_av, AV0)
            nc.vector.memset(mark[:, 9:10], 0.0).then_inc(s_lo, LO0)
            nc.vector.memset(mark[:, 10:11], 0.0).then_inc(s_op, OP0)
            nc.vector.memset(mark[:, 11:12], 0.0).then_inc(s_o, O0)
            nc.vector.memset(mark[:, 13:14], 0.0).then_inc(s_sum, SUM0)
            dve.wait_ge(s_va, NT)

            def front(i, b, s):
                at = placed(i, b, s)
                if at:
                    i1, b1, s1 = at
                    dve.wait_ge(s_s, step(i1, b1, s1 + 1))
                    nc.vector.tensor_reduce(nmax[:, s1 % 8:s1 % 8 + 1], bank(2 * ring_slot(s1), 2), AX.X, ALU.max,
                                            negate=True).then_inc(s_max, 1)

                def values(i, b, s):
                    return V[:, b * MT + s % MT, bass.ds(i * (4 * VD) + s // MT * VD, VD)]

                one = placed(i, b, s - 1) if s >= 1 else None
                two = placed(i, b, s - 2) if s >= 2 else None
                if one:
                    i1, b1, s1 = one
                    c = s1 % 8
                    dve.wait_ge(s_exp, step(i1, b1, s1 + (1 + EXP0)))
                    nc.vector.reciprocal(rsum[:, c:c + 1], esum[:, c:c + 1]).then_inc(s_rs, 1)
                if two and not is_whole(two[2]):
                    i2, b2, s2 = two
                    c, n = s2 % 8, slot_of(s2)
                    dve.wait_ge(s_vsh, nth(i2, b2, s2) + 1)
                    nc.vector.scalar_tensor_tensor(vs[:, n, VD:2 * VD], values(i2, b2, s2), rsum[:, c:c + 1],
                                                   vs[:, n, 0:VD].bitcast(F32), ALU.mult,
                                                   ALU.subtract).then_inc(s_vsl, 1)
                if one:
                    c = s1 % 8
                    wait_slot(dve, i1, b1, s1)
                    dve.wait_ge(s_rs, step(i1, b1, s1 + 1))
                    if is_whole(s1):
                        dst, done = vsn[:, s1 // 4 % 2, :], s_vsn
                    else:
                        dst, done = vs[:, slot_of(s1), 0:VD], s_vsh
                    nc.vector.tensor_scalar(dst, values(i1, b1, s1), rsum[:, c:c + 1], None,
                                            ALU.mult).then_inc(done, 1)

            AHEAD = 6
            for s in range(AHEAD + 1):
                front(0, 0, s)

            def body(i, b):
                for s in range(STEPS):
                    if s % PST != 0:
                        front(i, b, s + AHEAD)
                    h = s // MT
                    if s % MT == MT - 1:
                        dve.wait_ge(s_op, head(i, b, h + (OP0 - 1)))
                        for half in range(2):
                            if half == 0:
                                dve.wait_ge(s_avh, head(i, b, h + 1))
                            else:
                                dve.wait_ge(s_av, step(i, b, s + (1 + AV0)))
                            nc.vector.tensor_copy(oT[:, h % 2, half * 512:(half + 1) * 512],
                                                  bank(6 + half)).then_inc(s_o, 1)
                    if s % PST == PST - 1:
                        front(i, b, s + AHEAD + 1)
                        dve.wait_ge(s_op, head(i, b, h + (1 + OP0)))
                        dve.wait_ge(s_sum, pair(i, b, s // PST) + SUM0)
                        a = aT[:, b * N:(b + 1) * N]
                        nc.vector.tensor_tensor(a, a, bank(2 * OUT_SLOT, 2), ALU.add).then_inc(s_sum, 1)
            dve.wait_ge(s_a0, 1)
            for b in range(B):
                quads(dve, b, body)

        def att_pool(pool):
            pool.wait_ge(s_whi, 1)
            nc.gpsimd.tensor_tensor(wqklo[:, :], wqkraw[:, :], wqkhi[:, :].bitcast(F32), ALU.subtract).then_inc(s_wlo, 1)
            pool.wait_ge(s_whi, 2)
            nc.gpsimd.tensor_tensor(wvlo[:, :], wvraw[:, :], wvhi[:, :].bitcast(F32), ALU.subtract).then_inc(s_wlo, 1)
            nc.gpsimd.memset(ks[:, :, :, :].bitcast(F32), 0.0).then_inc(s_k0, 1)
            nc.gpsimd.memset(aT[:, :], 0.0).then_inc(s_a0, 1)

            def body(i, b):
                for s in range(STEPS):
                    if not is_whole(s):
                        n = slot_of(s)
                        pool.wait_ge(s_hi, nth(i, b, s) + 1)
                        wait_slot(pool, i, b, s)
                        nc.gpsimd.tensor_tensor(elo[:, n, :], ef[:, n, :], ehi[:, n, :].bitcast(F32),
                                                ALU.subtract).then_inc(s_lo, 1)
            for b in range(B):
                quads(pool, b, body)

        block = ctx.enter_context(nc.Block())

        @block.sync
        def _(sp):
            sp.dma_start(xt[:, 0:TPG, :], x_v[0]).then_inc(s_x[0], 16)
            sp.dma_start(consts[:, :], cst).then_inc(s_cst, 16)
            for g in range(1, GR):
                sp.dma_start(xt[:, g * TPG:(g + 1) * TPG, :], x_v[g]).then_inc(s_x[g], 16)
            sp.dma_start(wr_sb[:, :], wr).then_inc(s_cst, 16)
            sp.dma_start(br_sb[:, :], br.unsqueeze(0).broadcast_to([P, E])).then_inc(s_cst, 16)
            sp.dma_start(b2_sb[:, :], b2).then_inc(s_cst, 16)
            ffn_sync(sp, ffns[0])
            att_sync(sp)
            sp.wait_ge(s_sum, B * PAIRS + SUM0)
            for u in range(4):
                sp.wait_ge(s_st[u], 32 * len(UNITS) // 4)
            sp.wait_ge(norms[2].res, GR)
            ffn_sync(sp, ffns[1])
            for g in range(GR):
                sp.wait_ge(norms[3].res, g + 1)
                sp.dma_start(out_v[g], xt[:, g * TPG:(g + 1) * TPG, :]).then_inc(s_out, 16)
            sp.wait_ge(s_out, 16 * GR)
            for F in ffns:
                sp.wait_ge(F.gd, 16)

        @block.gpsimd
        def _(pool):
            nc.gpsimd.memset(mhalf[:, :], -0.5).then_inc(s_fill, 1)
            pool.wait_ge(s_fill, 1)
            norm_pool(pool, norms[0])
            ffn_pool(pool, ffns[0])
            norm_pool(pool, norms[1])
            att_pool(pool)
            norm_pool(pool, norms[2])
            ffn_pool(pool, ffns[1])

        @block.scalar
        def _(act):
            act.wait_ge(s_cst, 64)
            norm_act(act, norms[0])
            ffn_act(act, ffns[0])
            norm_act(act, norms[1])
            att_act(act)
            norm_act(act, norms[2])
            ffn_act(act, ffns[1])

        @block.vector
        def _(dve):
            dve.wait_ge(s_cst, 64)
            norm_dve(dve, norms[0])
            ffn_dve(dve, ffns[0])
            norm_dve(dve, norms[1])
            att_dve(dve)
            norm_dve(dve, norms[2])
            ffn_dve(dve, ffns[1])
            for g in range(GR):
                residual_dve(dve, norms[3], g)

        @block.tensor
        def _(pe):
            pe.wait_ge(s_cst, 64)
            norm_pe(pe, norms[0])
            ffn_pe(pe, ffns[0])
            pe.wait_ge(ffns[0].acc, A0 + GR * E)
            norm_pe(pe, norms[1])
            att_pe(pe)
            pe.wait_ge(s_sum, B * PAIRS + SUM0)
            norm_pe(pe, norms[2])
            ffn_pe(pe, ffns[1])
            pe.wait_ge(ffns[1].acc, A0 + GR * E)
            for g in range(GR):
                back_pe(pe, norms[3], g)


def kernel(L0_attn_x, L0_attn_query_proj, L0_attn_key_proj, L0_attn_value_proj, L0_attn_output_proj,
           L0_ffn_Wr, L0_ffn_br, L0_ffn_W1, L0_ffn_b1, L0_ffn_W2, L0_ffn_b2):
    import numpy as np
    import concourse.bacc as bacc
    from concourse.bass_utils import run_bass_kernel_spmd

    query = np.asarray(L0_attn_query_proj).reshape(KD, H, D).transpose(1, 0, 2)
    key = np.asarray(L0_attn_key_proj)
    consts = np.zeros((P, C_W), np.float32)
    consts[:, C_ID:C_ID + P] = np.eye(P)
    consts[:, C_TIE:] = np.tril(np.ones((E, E)), -1).reshape(-1)

    arrays = {
        "x": L0_attn_x,
        "cst": consts,
        "wqk": np.concatenate([query.reshape(H * KD, D), key.reshape(H * KD, D)]).T,
        "wv": np.asarray(L0_attn_value_proj).reshape(H * VD, D).T,
        "wo": np.asarray(L0_attn_output_proj).transpose(1, 2, 0),
        "wr": L0_ffn_Wr,
        "br": L0_ffn_br,
        "w1": L0_ffn_W1,
        "b1": np.asarray(L0_ffn_b1).reshape(E, MC, P).transpose(0, 2, 1),
        "w2": np.asarray(L0_ffn_W2).reshape(E, MC, P, D).transpose(0, 2, 1, 3).reshape(E, P, MC * D),
        "b2": np.asarray(L0_ffn_b2).T,
    }
    nc = bacc.Bacc("TRN2", target_bir_lowering=False, num_devices=1)
    feed, args = {}, []
    for name, a in arrays.items():
        a = np.ascontiguousarray(a)
        feed[f"in_{name}"] = a
        args.append(nc.dram_tensor(f"in_{name}", a.shape, F32, kind="ExternalInput").ap())
    args.append(nc.dram_tensor("out_0", (B, N, D), F32, kind="ExternalOutput").ap())
    macaron_kernel(nc, *args)
    return run_bass_kernel_spmd(nc, [feed], core_ids=[0]).results[0]["out_0"]
```

```python
import concourse.bass as bass
from concourse import mybir
from contextlib import ExitStack

F32 = mybir.dt.float32
F32R = mybir.dt.float32r
ALU = mybir.AluOpType
ACT = mybir.ActivationFunctionType
AX = mybir.AxisListType

P = 128
D = 128
B, N = 2, 1024
TOK = B * N
NT = TOK // P
GR = TOK // 512
TPG = NT // GR
E, M = 8, 512
MC = M // P
H, KD, VD = 16, 16, 64
QUAD = 4
QUADS = H // QUAD
MT = N // P
LN_EPS = 1e-5
EPS = 1e-9
SCALE = float(KD) ** -0.5
PARTS = 4

C_ID, C_PRI = 0, P
C_W = P + E


def macaron_kernel(nc, x, cst, wqk, wv, wo, wr, br, w1, b1, w2, b2, out):
    ctx = ExitStack()
    with ctx:
        def sem(name):
            return ctx.enter_context(nc.semaphore(name))

        def sb(name, shape, dt, stack=ctx):
            return stack.enter_context(nc.sbuf_tensor(name, shape, dt))

        ps = ctx.enter_context(nc.psum_tensor("ps", [P, 8 * 512], F32))

        def bank(b, n=1):
            return ps[:, b * 512:(b + n) * 512]

        xt = sb("xt", [P, NT, D], F32)
        heads_out = ExitStack()
        oT = sb("oT", [P, 4, N], F32, heads_out)
        heads_out.close()
        xhi = sb("xhi", [P, TOK], F32R)
        xlo = sb("xlo", [P, TOK], F32R)
        xn = sb("xn", [P, 2, TPG, D], F32)
        consts = sb("consts", [P, C_W], F32)
        ident = consts[:, C_ID:C_ID + P]
        priority = consts[:, C_PRI:C_PRI + E]
        stats = sb("stats", [P, NT, 6], F32)
        mv = sb("mv", [P, NT, 2], F32)
        rstd = sb("rstd", [P, NT], F32)
        mark = sb("mark", [P, 14], F32)
        mhalf = sb("mhalf", [P, TPG], F32)
        wr_sb = sb("wr_sb", [P, E], F32)
        br_sb = sb("br_sb", [P, E], F32)
        b1_sb = sb("b1_sb", [P, 2, MC], F32)
        b2_sb = sb("b2_sb", [P, E], F32)

        ffn = ExitStack()
        xf = sb("xf", [P, TOK], F32, ffn)
        w1raw = sb("w1raw", [P, 2, M], F32, ffn)
        w2raw = sb("w2raw", [P, 2, MC * D], F32, ffn)
        w1hi = sb("w1hi", [P, 2, M], F32R, ffn)
        w1lo = sb("w1lo", [P, 2, M], F32R, ffn)
        w2hi = sb("w2hi", [P, 2, MC * D], F32R, ffn)
        w2lo = sb("w2lo", [P, 2, MC * D], F32R, ffn)
        gb = sb("gb", [P, 2, TOK], F32, ffn)
        hf = sb("hf", [P, MC, 512], F32, ffn)
        hhi = sb("hhi", [P, 2, MC, 512], F32R, ffn)
        hlo = sb("hlo", [P, 2, MC, 512], F32R, ffn)
        ysc = sb("ysc", [P, 2, 512], F32, ffn)
        pr = sb("pr", [P, NT, E], F32, ffn)
        gw = sb("gw", [P, NT, E], F32, ffn)
        pick = sb("pick", [P, 2, NT, E], F32, ffn)
        rest = sb("rest", [P, NT, E], F32, ffn)
        rcol = sb("rcol", [P, NT], F32, ffn)
        col = sb("col", [P, NT], F32, ffn)
        gte = sb("gte", [P, E, NT], F32, ffn)
        gT = sb("gT", [P, P], F32, ffn)
        acc = sb("acc", [P, TOK], F32, ffn)
        ffn.close()

        RING = 4
        att = ExitStack()
        V = sb("V", [P, NT, H * VD], F32, att)
        qs = sb("qs", [P, 2, N], F32R, att)
        wo_sb = sb("wo_sb", [P, 4, D], F32, att)
        nmax = sb("nmax", [P, 8], F32, att)
        esum = sb("esum", [P, 8], F32, att)
        rsum = sb("rsum", [P, 8], F32, att)
        aT = sb("aT", [P, TOK], F32, att)
        vs = sb("vs", [P, RING, 2 * VD], F32R, att)
        vsn = sb("vsn", [P, RING, VD], F32, att)
        efn = sb("efn", [P, RING, N], F32, att)
        ef = sb("ef", [P, RING, N], F32, att)
        vq = sb("vq", [P, 2, MT, 2 * VD], F32, att)
        ks = sb("ks", [P, 2, 2, N], F32R, att)
        early = ExitStack()
        sthi = sb("sthi", [P, 4, 512], F32R, early)
        stlo = sb("stlo", [P, 4, 512], F32R, early)
        wqkraw = sb("wqkraw", [P, 4 * P], F32, early)
        wqkhi = sb("wqkhi", [P, 4 * P], F32R, early)
        wqklo = sb("wqklo", [P, 4 * P], F32R, early)
        wvraw = sb("wvraw", [P, H * VD], F32, early)
        wvhi = sb("wvhi", [P, H * VD], F32R, early)
        wvlo = sb("wvlo", [P, H * VD], F32R, early)
        early.close()
        ehi = sb("ehi", [P, RING, N], F32R, att)
        elo = sb("elo", [P, RING, N], F32R, att)
        att.close()

        qkd = nc.dram_tensor("qk_parts", [2, H, 2, KD, TOK], F32, kind="Internal").ap()
        gd = [nc.dram_tensor(f"gates{f}", [P, P], F32, kind="Internal").ap() for f in range(2)]

        x_v = x.rearrange("b n d -> (b n) d").rearrange("(g t p) d -> g p t d", g=GR, p=P)
        out_v = out.rearrange("b n d -> (b n) d").rearrange("(g t p) d -> g p t d", g=GR, p=P)

        s_x = [sem(f"s_x{g}") for g in range(GR)]
        s_cst = sem("s_cst")
        s_fill = sem("s_fill")
        s_out = sem("s_out")

        class Norm:
            def __init__(self, k, src):
                self.k, self.src = k, src
                self.back = sem(f"n{k}_back")
                self.res = sem(f"n{k}_res")
                self.st = sem(f"n{k}_st")
                self.mv = sem(f"n{k}_mv")
                self.eps = sem(f"n{k}_eps")
                self.rstd = sem(f"n{k}_rstd")
                self.xn = sem(f"n{k}_xn")
                self.fwd = sem(f"n{k}_fwd")
                self.x32 = sem(f"n{k}_x32")
                self.hi = sem(f"n{k}_hi")
                self.lo = sem(f"n{k}_lo")

        norms = [Norm(0, None), Norm(1, acc), Norm(2, aT), Norm(3, acc)]

        def back_bank(n, g):
            return g % 2 if n.k == 2 else (4, 5, 0, 1)[g]

        def back_pe(pe, n, g):
            if n.k == 2 and g >= 2:
                pe.wait_ge(n.res, g - 1)
            for t in range(TPG):
                at = (g * TPG + t) * P
                last = nc.tensor.transpose(bank(back_bank(n, g))[:, t * P:(t + 1) * P], n.src[:, at:at + P], ident)
            last.then_inc(n.back, 1)

        def residual_dve(dve, n, g):
            dve.wait_ge(n.back, g + 1)
            xg = xt[:, g * TPG:(g + 1) * TPG, :]
            nc.vector.tensor_tensor(xg, xg, bank(back_bank(n, g)).rearrange("p (t d) -> p t d", d=D),
                                    ALU.add).then_inc(n.res, 1)

        def forward_pe(pe, n, g):
            pe.wait_ge(n.xn, g + 1)
            if g >= 2:
                pe.wait_ge(n.lo, g - 1)
            for t in range(TPG):
                last = nc.tensor.transpose(bank(6 + g % 2)[:, t * P:(t + 1) * P], xn[:, g % 2, t, :], ident)
            last.then_inc(n.fwd, 1)

        def norm_pe(pe, n, F):
            for g in range(GR + 1):
                if n.k == 2 and g < 2:
                    pe.wait_ge(s_sum, B * QUADS * OUTS + SUM0 - 1 + g)
                    back_pe(pe, n, g + 2)
                if g < GR:
                    forward_pe(pe, n, g)
                if g > 0:
                    logits_pe(pe, F, g - 1)

        def high_act(act, n, g):
            cols = slice(g * 512, (g + 1) * 512)
            act.wait_ge(n.fwd, g + 1)
            if n.k != 1:
                nc.scalar.activation(xf[:, cols], bank(6 + g % 2), ACT.Copy).then_inc(n.x32, 1)
            nc.scalar.activation(xhi[:, cols], bank(6 + g % 2), ACT.Copy).then_inc(n.hi, 1)

        def norm_act(act, n):
            for g in range(GR):
                high_act(act, n, g)

        def norm_pool(pool, n):
            for g in range(GR):
                r = rstd[:, g * TPG:(g + 1) * TPG]
                pool.wait_ge(n.mv, g + 1)
                nc.gpsimd.tensor_scalar(r, mv[:, g * TPG:(g + 1) * TPG, 1], LN_EPS, None, ALU.add).then_inc(n.eps, 1)
                pool.wait_ge(n.eps, g + 1)
                nc.gpsimd.tensor_tensor(r, r, mhalf[:, :], ALU.pow).then_inc(n.rstd, 1)

        def statistics_dve(dve, n, g):
            if n.src is None:
                dve.wait_ge(s_x[g], 16)
            else:
                residual_dve(dve, n, g)
                dve.wait_ge(n.res, g + 1)
            for t in range(g * TPG, (g + 1) * TPG):
                last = nc.vector.bn_stats(stats[:, t, :], xt[:, t, :])
            last.then_inc(n.st, 1)
            dve.wait_ge(n.st, g + 1)
            for t in range(g * TPG, (g + 1) * TPG):
                last = nc.vector.bn_aggr(mv[:, t, :], stats[:, t, :])
            last.then_inc(n.mv, 1)

        def scaled_dve(dve, n, g):
            dve.wait_ge(n.rstd, g + 1)
            if g >= 2:
                dve.wait_ge(n.fwd, g - 1)
            for t in range(TPG):
                a = g * TPG + t
                last = nc.vector.tensor_scalar(xn[:, g % 2, t, :], xt[:, a, :], mv[:, a, 0:1], rstd[:, a:a + 1],
                                               ALU.subtract, ALU.mult)
            last.then_inc(n.xn, 1)

        def low_dve(dve, n, g):
            cols = slice(g * 512, (g + 1) * 512)
            dve.wait_ge(n.hi, g + 1)
            nc.vector.tensor_tensor(xlo[:, cols], bank(6 + g % 2), xhi[:, cols].bitcast(F32),
                                    ALU.subtract).then_inc(n.lo, 1)

        def norm_dve(dve, n):
            done = 2 if n.k == 2 else 0
            for g in range(done, GR + 2):
                if g < GR:
                    statistics_dve(dve, n, g)
                if done <= g - 1 < GR:
                    scaled_dve(dve, n, g - 1)
                if g >= 2:
                    low_dve(dve, n, g - 2)

        class Ffn:
            def __init__(self, f, n, after):
                self.f, self.n, self.after = f, n, after
                self.logit = sem(f"f{f}_logit")
                self.sh = sem(f"f{f}_sh")
                self.ex = sem(f"f{f}_ex")
                self.lg = sem(f"f{f}_lg")
                self.chain = sem(f"f{f}_chain")
                self.g = sem(f"f{f}_g")
                self.gT = sem(f"f{f}_gT")
                self.gTs = sem(f"f{f}_gTs")
                self.gd = sem(f"f{f}_gd")
                self.acc0 = sem(f"f{f}_acc0")
                self.whi = sem(f"f{f}_whi")
                self.wready = sem(f"f{f}_wready")
                self.h = sem(f"f{f}_h")
                self.gelu = sem(f"f{f}_gelu")
                self.hi = sem(f"f{f}_hi")
                self.lo = sem(f"f{f}_lo")
                self.y = sem(f"f{f}_y")
                self.scaled = sem(f"f{f}_scaled")
                self.acc = sem(f"f{f}_acc")
                self.w = [sem(f"f{f}_w{u}") for u in range(2)]
                self.gb = [sem(f"f{f}_gb{u}") for u in range(2)]
                self.b1 = [sem(f"f{f}_b1{u}") for u in range(2)]

        ffns = [Ffn(0, norms[0], norms[1]), Ffn(1, norms[2], norms[3])]

        Y0 = A0 = 2
        S0 = L0 = 4
        SKEW = 3

        def load_expert(q, F, e, u):
            q.dma_start(w1raw[:, u, :], w1[bass.ds(e, 1), :, :].rearrange("a p n -> (a p) n")).then_inc(F.w[u], 16)
            q.dma_start(w2raw[:, u, :], w2[bass.ds(e, 1), :, :].rearrange("a p n -> (a p) n")).then_inc(F.w[u], 16)

        def load_gates(q, F, e, u):
            src = gd[F.f].rearrange("a b -> (a b)").rearrange("(e n) -> e n", e=E)[bass.ds(e, 1), :]
            q.dma_start(gb[:, u, :], src.broadcast_to([P, TOK])).then_inc(F.gb[u], 16)

        def load_bias(q, F, e, u):
            q.dma_start(b1_sb[:, u, :], b1[bass.ds(e, 1), :, :].rearrange("a p n -> (a p) n")).then_inc(F.b1[u], 16)

        def first_weights_sync(sp, F):
            for e in range(2):
                load_expert(sp, F, e, e)
                load_bias(sp, F, e, e)

        def first_weights_act(act, F):
            act.wait_ge(F.w[0], 32)
            high_weights(F, 0)

        def first_weights_pool(pool, F):
            pool.wait_ge(F.whi, 1)
            low_weights(F, 0)

        def high_weights(F, u):
            nc.scalar.activation(w1hi[:, u, :], w1raw[:, u, :], ACT.Copy)
            nc.scalar.activation(w2hi[:, u, :], w2raw[:, u, :], ACT.Copy).then_inc(F.whi, 1)

        def low_weights(F, u):
            nc.gpsimd.tensor_tensor(w1lo[:, u, :], w1raw[:, u, :], w1hi[:, u, :].bitcast(F32), ALU.subtract)
            nc.gpsimd.tensor_tensor(w2lo[:, u, :], w2raw[:, u, :], w2hi[:, u, :].bitcast(F32),
                                    ALU.subtract).then_inc(F.wready, 1)

        def ffn_sync(sp, F):
            sp.wait_ge(F.gTs, 1)
            sp.dma_start(gd[F.f], gT[:, :]).then_inc(F.gd, 16)
            sp.wait_ge(F.gd, 16)
            for e in range(2):
                load_gates(sp, F, e, e)
            with sp.Fori(0, E // 2 - 1) as i:
                for u in range(2):
                    sp.wait_ge(F.wready, i * 2 + (u + 1))
                    load_expert(sp, F, i * 2 + (u + 2), u)
                for u in range(2):
                    sp.wait_ge(F.gelu, i * 32 + 16 * (u + 1))
                    load_bias(sp, F, i * 2 + (u + 2), u)
                    sp.wait_ge(F.scaled, i * 8 + (S0 + 4 * (u + 1)))
                    load_gates(sp, F, i * 2 + (u + 2), u)

        def ffn_units(eng, body):
            body(0, True, False)
            with eng.Fori(1, E // 2 - 1) as i:
                body(i, False, False)
            body(E // 2 - 1, False, True)

        def next_expert(i, s):
            return s % GR == 0 and not (isinstance(i, int) and i == E // 2 - 1 and s >= GR)

        def logits_pe(pe, F, g):
            pe.wait_ge(F.n.x32, g + 1)
            for t in range(g * TPG, (g + 1) * TPG):
                last = nc.tensor.matmul(bank(5)[:, t * E:(t + 1) * E], xf[:, t * P:(t + 1) * P], wr_sb[:, :],
                                        start=True, stop=True)
            last.then_inc(F.logit, 1)

        def ffn_pe(pe, F):
            pe.wait_ge(F.n.lo, GR)

            def hidden(i, s, mc):
                u, tt = (s // GR) % 2, s % GR
                if tt == 0 and mc == 0:
                    pe.wait_ge(F.wready, i * 2 + (s // GR + 1))
                if not (isinstance(i, int) and i == 0 and s == 0):
                    pe.wait_ge(F.gelu, i * 32 + (4 * s + mc - 3))
                w = slice(mc * P, (mc + 1) * P)
                cols = slice(tt * 512, (tt + 1) * 512)
                nc.tensor.matmul(bank(mc), w1lo[:, u, w], xhi[:, cols], start=True, stop=False)
                nc.tensor.matmul(bank(mc), w1hi[:, u, w], xlo[:, cols], start=False, stop=False)
                nc.tensor.matmul(bank(mc), w1hi[:, u, w], xhi[:, cols], start=False, stop=True).then_inc(F.h, 1)

            def output(i, s, mc):
                u, tt = s // GR, s % GR
                if mc == 0:
                    pe.wait_ge(F.scaled, i * 8 + (s + S0 - 3))
                pe.wait_ge(F.lo, i * 32 + (4 * s + mc + 1 + L0))
                w = slice(mc * D, (mc + 1) * D)
                y = bank(4 + s % 4)
                nc.tensor.matmul(y, w2lo[:, u, w], hhi[:, s % 2, mc, :], start=(mc == 0), stop=False)
                nc.tensor.matmul(y, w2hi[:, u, w], hlo[:, s % 2, mc, :], start=False, stop=False)
                last = nc.tensor.matmul(y, w2hi[:, u, w], hhi[:, s % 2, mc, :], start=False, stop=(mc == MC - 1))
                if mc == MC - 1:
                    last.then_inc(F.y, 1)

            for mc in range(MC):
                hidden(0, 0, mc)

            def body(i, first, last):
                for s in range(2 * GR):
                    if first and s == 2:
                        pe.wait_ge(F.g, 1)
                        nc.tensor.transpose(bank(7)[:, 0:P], gte[:, :, :].rearrange("p e t -> p (e t)"),
                                            ident).then_inc(F.gT, 1)
                    for mc in range(MC):
                        if not (last and s == 2 * GR - 1):
                            hidden(i, s + 1, mc)
                        if first and s == 3 and mc == 0:
                            pe.wait_ge(F.gTs, 1)
                        output(i, s, mc)
            ffn_units(pe, body)
            pe.wait_ge(F.gelu, GR * E * MC)
            for g in range(GR):
                pe.wait_ge(F.acc, A0 + GR * (E - 1) + g + 1)
                back_pe(pe, F.after, g)

        def ffn_act(act, F):
            act.wait_ge(F.sh, 1)
            nc.scalar.activation(pr[:, :, :], pr[:, :, :], ACT.Exp).then_inc(F.ex, 1)

            def front(i, s):
                u = s // GR % 2
                if s % GR == 0:
                    act.wait_ge(F.b1[u], i * 16 + (s // (2 * GR) + 1) * 16)
                for mc in range(MC):
                    act.wait_ge(F.h, i * 32 + (4 * s + mc + 1))
                    act.wait_ge(F.lo, i * 32 + (4 * s + mc + 1))
                    nc.scalar.activation(hf[:, mc, :], bank(mc), ACT.Gelu,
                                         bias=b1_sb[:, u, mc:mc + 1]).then_inc(F.gelu, 1)

            def back(i, s):
                if next_expert(i, s):
                    u = (s // GR + 1) % 2
                    e = i * 2 + s // GR
                    act.wait_ge(F.y, e * 4 + Y0)
                    act.wait_ge(F.w[u], (i + (s // GR + 1) // 2) * 32 + 32)
                    high_weights(F, u)

            def body(i, first, last):
                for s in range(2 * GR):
                    if not (last and s == 2 * GR - 1):
                        front(i, s + 1)
                    back(i, s)
            front(0, 0)
            ffn_units(act, body)

        def ffn_pool(pool, F):
            nc.gpsimd.memset(acc[:, :], 0.0).then_inc(F.acc0, 1)
            if F.f == 0:
                first_weights_pool(pool, F)
                att_weights_pool(pool)

            def body(i, first, last):
                for s in range(2 * GR):
                    tt = s % GR
                    pool.wait_ge(F.scaled, i * 8 + (s + 1 + S0))
                    a = acc[:, tt * 512:(tt + 1) * 512]
                    nc.gpsimd.tensor_tensor(a, a, ysc[:, s % 2, :], ALU.add).then_inc(F.acc, 1)
                    if tt == GR - 2 and not last:
                        pool.wait_ge(F.whi, i * 2 + (s // GR + 3))
                        low_weights(F, s // GR)
            pool.wait_ge(F.whi, 2)
            low_weights(F, 1)
            pool.wait_ge(F.acc0, 1)
            ffn_units(pool, body)

        def ffn_dve(dve, F):
            dve.wait_ge(F.logit, GR)
            nc.vector.tensor_tensor(pr[:, :, :], bank(5)[:, 0:NT * E].rearrange("p (t e) -> p t e", e=E),
                                    br_sb[:, :].unsqueeze(1).broadcast_to([P, NT, E]), ALU.add).then_inc(F.lg, 1)
            dve.wait_ge(F.lg, 1)
            nc.vector.tensor_reduce(col[:, :], pr[:, :, :], AX.X, ALU.max).then_inc(F.lg, 1)
            dve.wait_ge(F.lg, 2)
            nc.vector.tensor_tensor(pr[:, :, :], pr[:, :, :], col[:, :].unsqueeze(2).broadcast_to([P, NT, E]),
                                    ALU.subtract).then_inc(F.sh, 1)
            nc.vector.memset(mark[:, 0 + 4 * F.f:1 + 4 * F.f], 0.0).then_inc(F.scaled, S0)
            nc.vector.memset(mark[:, 1 + 4 * F.f:2 + 4 * F.f], 0.0).then_inc(F.acc, A0)
            nc.vector.memset(mark[:, 2 + 4 * F.f:3 + 4 * F.f], 0.0).then_inc(F.y, Y0)
            nc.vector.memset(mark[:, 3 + 4 * F.f:4 + 4 * F.f], 0.0).then_inc(F.lo, L0)

            def router():
                count = [0]

                def link(ins):
                    count[0] += 1
                    ins.then_inc(F.chain, 1)

                def linked():
                    dve.wait_ge(F.chain, count[0])

                def over(t):
                    return t.unsqueeze(2).broadcast_to([P, NT, E])

                dve.wait_ge(F.ex, 1)
                link(nc.vector.tensor_reduce(col[:, :], pr[:, :, :], AX.X, ALU.add))
                yield
                linked()
                link(nc.vector.reciprocal(rcol[:, :], col[:, :]))
                yield
                linked()
                link(nc.vector.tensor_tensor(pr[:, :, :], pr[:, :, :], over(rcol[:, :]), ALU.mult))
                for k in range(2):
                    src = (pr, rest)[k]
                    one = pick[:, k, :, :]
                    yield
                    linked()
                    link(nc.vector.tensor_reduce(col[:, :], src[:, :, :], AX.X, ALU.max))
                    yield
                    linked()
                    link(nc.vector.tensor_tensor(one, src[:, :, :], over(col[:, :]), ALU.is_equal))
                    yield
                    linked()
                    link(nc.vector.tensor_tensor(gw[:, :, :], one, priority.unsqueeze(1).broadcast_to([P, NT, E]),
                                                 ALU.mult))
                    yield
                    linked()
                    link(nc.vector.tensor_reduce(col[:, :], gw[:, :, :], AX.X, ALU.max))
                    yield
                    linked()
                    link(nc.vector.tensor_tensor(one, gw[:, :, :], over(col[:, :]), ALU.is_equal))
                    if k == 0:
                        yield
                        linked()
                        link(nc.vector.scalar_tensor_tensor(rest[:, :, :], one, -2.0, pr[:, :, :], ALU.mult, ALU.add))
                yield
                linked()
                link(nc.vector.tensor_tensor(gw[:, :, :], pick[:, 0, :, :], pick[:, 1, :, :], ALU.add))
                yield
                linked()
                link(nc.vector.tensor_tensor(gw[:, :, :], gw[:, :, :], pr[:, :, :], ALU.mult))
                for last in range(2):
                    yield
                    linked()
                    link(nc.vector.tensor_reduce(col[:, :], gw[:, :, :], AX.X, ALU.add))
                    yield
                    linked()
                    link(nc.vector.tensor_scalar(col[:, :], col[:, :], EPS, None, ALU.add))
                    yield
                    linked()
                    link(nc.vector.reciprocal(rcol[:, :], col[:, :]))
                    yield
                    linked()
                    if not last:
                        link(nc.vector.tensor_tensor(gw[:, :, :], gw[:, :, :], over(rcol[:, :]), ALU.mult))
                nc.vector.scalar_tensor_tensor(gte[:, :, :].rearrange("p e t -> p t e"), gw[:, :, :], 0.5,
                                               over(rcol[:, :]), ALU.mult, ALU.mult).then_inc(F.g, 1)

            def front(i, s, gates=iter(())):
                dve.wait_ge(F.y, i * 8 + (s + Y0 - 1))
                for mc in range(MC):
                    dve.wait_ge(F.gelu, i * 32 + (4 * s + mc + 1))
                    nc.vector.tensor_copy(hhi[:, s % 2, mc, :], hf[:, mc, :]).then_inc(F.hi, 1)
                    next(gates, None)
                    dve.wait_ge(F.hi, i * 32 + (4 * s + mc + 1))
                    nc.vector.tensor_tensor(hlo[:, s % 2, mc, :], hf[:, mc, :], hhi[:, s % 2, mc, :].bitcast(F32),
                                            ALU.subtract).then_inc(F.lo, 1)
                    next(gates, None)

            def back(i, s):
                u, tt = s // GR, s % GR
                if tt == 0:
                    dve.wait_ge(F.gb[u], i * 16 + 16)
                dve.wait_ge(F.y, i * 8 + (s + 1 + Y0))
                dve.wait_ge(F.acc, i * 8 + (s + A0 - 1))
                nc.vector.scalar_tensor_tensor(ysc[:, s % 2, :], bank(4 + s % 4), b2_sb[:, bass.ds(i * 2 + u, 1)],
                                               gb[:, u, tt * 512:(tt + 1) * 512], ALU.add,
                                               ALU.mult).then_inc(F.scaled, 1)

            def body(i, first, last):
                for s in range(2 * GR):
                    if not (last and s + SKEW >= 2 * GR):
                        front(i, s + SKEW)
                    back(i, s)
            gates = router()
            for _ in range(3):
                next(gates)
            for s in range(SKEW):
                front(0, s, gates)
            for _ in gates:
                pass
            dve.wait_ge(F.gT, 1)
            nc.vector.tensor_copy(gT[:, :], bank(7)[:, 0:P]).then_inc(F.gTs, 1)
            ffn_units(dve, body)

        s_wv = sem("s_wv")
        s_wqk = sem("s_wqk")
        s_whi = sem("s_whi")
        s_wlo = sem("s_wlo")
        s_qk = sem("s_qk")
        s_qkhi = sem("s_qkhi")
        s_qklo = sem("s_qklo")
        s_st = [sem(f"s_st{u}") for u in range(4)]
        s_v = sem("s_v")
        s_va = sem("s_va")
        s_vq = [sem(f"s_vq{u}") for u in range(2)]
        s_k0 = sem("s_k0")
        s_a0 = sem("s_a0")
        s_pair = [sem(f"s_pair{u}") for u in range(2)]
        s_wo = [sem(f"s_wo{u}") for u in range(2)]
        s_s = sem("s_s")
        s_max = sem("s_max")
        s_exp = sem("s_exp")
        s_hi = sem("s_hi")
        s_lo = sem("s_lo")
        s_rs = sem("s_rs")
        s_vsh = sem("s_vsh")
        s_vsl = sem("s_vsl")
        s_vsn = sem("s_vsn")
        s_av = sem("s_av")
        s_avh = sem("s_avh")
        s_o = sem("s_o")
        s_op = sem("s_op")
        s_sum = sem("s_sum")

        EXP0, LO0, AV0, O0, OP0, SUM0 = 3, RING, 16, 2, 4, 4
        STEPS = 4 * MT
        PST = 2 * MT
        CYCLE = 8
        WHOLE = [1, 4, 6]
        SPLIT = [r for r in range(CYCLE) if r not in WHOLE]

        def step(i, b, s):
            return i * STEPS + (b * QUADS * STEPS + s)

        def kind(s):
            return WHOLE if s % CYCLE in WHOLE else SPLIT

        def is_whole(s):
            return kind(s) is WHOLE

        def nth(i, b, s):
            n, per_quad = len(kind(s)), STEPS // CYCLE * len(kind(s))
            return i * per_quad + (b * QUADS * per_quad + s // CYCLE * n + kind(s).index(s % CYCLE))

        def slot_of(s):
            return nth(0, 0, s) % RING

        def wait_slot(eng, i, b, s):
            used = s - 1
            while kind(used) is not kind(s) or slot_of(used) != slot_of(s):
                used -= 1
            eng.wait_ge(s_av, step(i, b, used + (AV0 + 1)))

        LEAD = 6
        OUTS = STEPS // MT

        def ring_slot(s):
            r = s % STEPS
            return (r + sum(x < r for x in range(LEAD % MT, STEPS, MT))) % 3
        OUT_SLOT = (LEAD % MT + 1) % 3

        def out_bank(i, b, s):
            very_last = isinstance(i, int) and b == B - 1 and s == STEPS + 2 * MT - 1
            return 2 * (ring_slot(STEPS - 1) if very_last else OUT_SLOT)

        def out_number(i, b, s):
            return i * OUTS + (b * QUADS * OUTS + (s + 1) // MT - 3)

        ROTATED = range(2 * MT, STEPS + 2 * MT)

        def quads(eng, b, body):
            with eng.Fori(0, QUADS - 1) as i:
                body(i, b)
            body(QUADS - 1, b)

        def placed(i, b, s):
            if s >= STEPS and isinstance(i, int) and i == QUADS - 1:
                i, b, s = 0, b + 1, s - STEPS
            return (i, b, s) if b < B else None

        def head(i, b, h):
            return i * 4 + (b * H + h)

        V_BANKS = (4, 5, 0, 1)
        UNITS = [(what, hg, g) for g in range(GR) for what in range(2) for hg in range(2)]

        def att_sync(sp):
            def load_pair(b, j, u):
                cols = slice(b * N, (b + 1) * N)
                for hh in range(2):
                    for part in range(2):
                        rows = slice(hh * 64 + 2 * part * KD, hh * 64 + 2 * (part + 1) * KD)
                        src = qkd[0, bass.ds(j * 2 + hh, 1), part, :, cols].broadcast_to([2, KD, N])
                        sp.dma_start(qs[rows, u, :].bitcast(F32), src).then_inc(s_pair[u], 16)
                    rows = slice(hh * 64, hh * 64 + PARTS * KD)
                    src = qkd[1, bass.ds(j * 2 + hh, 1), :, :, cols].rearrange("a c k n -> (a c k) n")
                    src = src.unsqueeze(0).broadcast_to([2, 2 * KD, N])
                    sp.dma_start(ks[rows, u, hh, :].bitcast(F32), src).then_inc(s_pair[u], 16)

            def load_wo(j, u):
                for part in range(2):
                    sp.dma_start(wo_sb[part * VD:(part + 1) * VD, 2 * u:2 * u + 2, :],
                                 wo[bass.ds(j * 2, 2), :, :].rearrange("a v d -> v a d")).then_inc(s_wo[u], 16)

            def load_values(b, j, u):
                src = V[:, b * MT:(b + 1) * MT, bass.ds(j * (2 * VD), 2 * VD)]
                sp.dma_start(vq[:, u, :, :], src).then_inc(s_vq[u], 16)

            def stage(n):
                what, hg, g = UNITS[n]
                sp.wait_ge(s_qklo, n + 1)
                rows = slice(hg * 8, hg * 8 + 8)
                for part, st in enumerate((sthi, stlo)):
                    dst = qkd[what, rows, part, :, g * 512:(g + 1) * 512]
                    sp.dma_start(dst, st[:, n % 4, :].bitcast(F32)).then_inc(s_st[n % 4], 16)

            early_units = len(UNITS) * 3 // 4
            for n in range(early_units):
                stage(n)
            for u in range(4):
                sp.wait_ge(s_st[u], 32 * len(UNITS) // B // 4)
            sp.wait_ge(s_k0, 1)
            load_pair(0, 0, 0)
            for n in range(early_units, len(UNITS)):
                stage(n)
            load_pair(0, 1, 1)
            sp.wait_ge(s_va, NT)
            for p in range(2):
                load_values(0, p, p)
            for p in range(2):
                load_wo(p, p)
            for u in range(4):
                sp.wait_ge(s_st[u], 32 * len(UNITS) // 4)

            def body(i, b):
                wrapped = isinstance(i, int)
                if wrapped and b == B - 1:
                    return
                for u in range(2):
                    sp.wait_ge(s_s, step(i, b, (u + 1) * PST))
                    if wrapped:
                        load_pair(b + 1, u, u)
                    else:
                        load_pair(b, i * 2 + (u + 2), u)
                    sp.wait_ge(s_av, step(i, b, (u + 1) * PST + AV0))
                    if wrapped:
                        load_values(b + 1, u, u)
                    else:
                        load_values(b, i * 2 + (u + 2), u)
                for u in range(2):
                    sp.wait_ge(s_op, out_number(i, b, (2 * u + 4) * MT - 1) + (1 + OP0))
                    load_wo(u if wrapped else i * 2 + (u + 2), u)
            for b in range(B):
                quads(sp, b, body)

        def att_pe(pe):
            n = norms[1]
            for g in range(2):
                forward_pe(pe, n, g)
            pe.wait_ge(s_wlo, 2)
            def values(unit):
                t, half = divmod(unit, 2)
                if unit == 2:
                    pe.wait_ge(n.res, GR)
                if unit >= 4:
                    pe.wait_ge(s_va, unit - 3)
                w = slice(half * 512, (half + 1) * 512)
                cols = slice(t * P, (t + 1) * P)
                o = bank(V_BANKS[unit % 4])
                nc.tensor.matmul(o, xlo[:, cols], wvhi[:, w], start=True, stop=False)
                nc.tensor.matmul(o, xhi[:, cols], wvlo[:, w], start=False, stop=False)
                nc.tensor.matmul(o, xhi[:, cols], wvhi[:, w], start=False, stop=True).then_inc(s_v, 1)

            for u, (what, hg, g) in enumerate(UNITS):
                if what == 0 and hg == 0:
                    pe.wait_ge(n.lo, g + 1)
                if u >= 2:
                    pe.wait_ge(s_qklo, u - 1)
                cols = slice(g * 512, (g + 1) * 512)
                w = slice((what * 2 + hg) * P, (what * 2 + hg + 1) * P)
                o = bank(2 + u % 2)
                nc.tensor.matmul(o, wqklo[:, w], xhi[:, cols], start=True, stop=False)
                nc.tensor.matmul(o, wqkhi[:, w], xlo[:, cols], start=False, stop=False)
                nc.tensor.matmul(o, wqkhi[:, w], xhi[:, cols], start=False, stop=True).then_inc(s_qk, 1)
                values(u)
                if u % 4 == 1 and g < 2:
                    forward_pe(pe, n, g + 2)
            for unit in range(len(UNITS), 2 * NT):
                values(unit)
            pe.wait_ge(s_va, 2 * NT)
            pe.wait_ge(s_qklo, len(UNITS))

            def scores(i, b, s):
                if placed(i, b, s) is None:
                    return
                i, b, s = placed(i, b, s)
                p, r = divmod(s, PST)
                hh, m = divmod(r, MT)
                if r == 0:
                    pe.wait_ge(s_pair[p % 2], i * 96 + ((b * QUADS + p // 2) * 96 + 96))
                behind = (s - LEAD) % MT
                if behind == 3:
                    pe.wait_ge(s_sum, out_number(i, b, s - LEAD - 4) + (1 + SUM0))
                else:
                    back = 2 if behind in (1, 2) else 3
                    pe.wait_ge(s_exp, step(i, b, s + (EXP0 + 1 - back)))
                slot = ring_slot(s)
                for half in range(2):
                    last = nc.tensor.matmul(bank(2 * slot + half), ks[:, p % 2, hh, m * P:(m + 1) * P],
                                            qs[:, p % 2, half * 512:(half + 1) * 512], start=True, stop=True)
                last.then_inc(s_s, 1)

            def products(i, b, s):
                if placed(i, b, s) is None:
                    return
                i, b, s = placed(i, b, s)
                r = s % MT
                if is_whole(s):
                    pe.wait_ge(s_exp, step(i, b, s + (1 + EXP0)))
                    pe.wait_ge(s_vsn, nth(i, b, s) + 1)
                else:
                    pe.wait_ge(s_lo, nth(i, b, s) + (1 + LO0))
                    pe.wait_ge(s_vsl, nth(i, b, s) + 1)
                for half in range(2):
                    cols = slice(half * 512, (half + 1) * 512)
                    if r == 0:
                        pe.wait_ge(s_o, head(i, b, s // MT) * 2 + (half + 1))
                    if is_whole(s):
                        n = slot_of(s)
                        last = nc.tensor.matmul(bank(6 + half)[0:VD, :], vsn[:, n, :], efn[:, n, cols],
                                                start=False, stop=False)
                    else:
                        n = slot_of(s)
                        nc.tensor.matmul(bank(6 + half), vs[:, n, :], elo[:, n, cols], start=(r == 0), stop=False)
                        last = nc.tensor.matmul(bank(6 + half), vs[:, n, :], ehi[:, n, cols],
                                                start=False, stop=(r == MT - 1))
                    if half == 0 and r == MT - 1:
                        last.then_inc(s_avh, 1)
                last.then_inc(s_av, 1)

            def outproj(i, b, s):
                p, half = divmod((s + 1) // MT - 3, 2)
                n = out_number(i, b, s)
                used = s + LEAD - 1
                while placed(i, b, used) is None or 2 * ring_slot(used) != out_bank(i, b, s):
                    used -= 1
                pe.wait_ge(s_exp, step(i, b, used + (1 + EXP0)))
                if placed(i, b, s) is None and out_bank(i, b, s) == 2 * OUT_SLOT:
                    pe.wait_ge(s_sum, n + SUM0)
                pe.wait_ge(s_o, head(i, b, 2 * p + 1) * 2 + (half + 1 + O0))
                pe.wait_ge(s_wo[p], i * 32 + (b * QUADS + 1) * 32)
                for hh in range(2):
                    last = nc.tensor.matmul(bank(out_bank(i, b, s)), wo_sb[:, 2 * p + hh, :],
                                            oT[:, 2 * p + hh, half * 512:(half + 1) * 512],
                                            start=(hh == 0), stop=(hh == 1))
                last.then_inc(s_op, 1)

            def pe_step(i, b, s, out):
                if s % MT != 0:
                    scores(i, b, s + LEAD)
                elif out:
                    outproj(i, b, s - 1)
                products(i, b, s)
                if s % MT == MT - 1:
                    scores(i, b, s + LEAD + 1)

            for s in range(LEAD + 1):
                scores(0, 0, s)
            for s in range(2 * MT + 1):
                pe_step(0, 0, s, False)

            def body(i, b):
                last = isinstance(i, int) and b == B - 1
                for s in ROTATED:
                    if last and s + 1 == STEPS - 2:
                        pe.wait_ge(s_exp, step(i, b, STEPS - 1 + EXP0))
                        for g in range(2):
                            back_pe(pe, norms[2], g)
                    pe_step(i, b, s + 1, True)
            for b in range(B):
                quads(pe, b, body)

        def att_weights_sync(sp):
            sp.dma_start(wqkraw[:, :], wqk).then_inc(s_wqk, 16)
            sp.dma_start(wvraw[:, :], wv).then_inc(s_wv, 16)

        def att_weights_act(act):
            act.wait_ge(s_wqk, 16)
            nc.scalar.activation(wqkhi[:, :], wqkraw[:, :], ACT.Copy).then_inc(s_whi, 1)
            act.wait_ge(s_wv, 16)
            nc.scalar.activation(wvhi[:, :], wvraw[:, :], ACT.Copy).then_inc(s_whi, 1)

        def att_weights_pool(pool):
            pool.wait_ge(s_whi, 1)
            nc.gpsimd.tensor_tensor(wqklo[:, :], wqkraw[:, :], wqkhi[:, :].bitcast(F32), ALU.subtract).then_inc(s_wlo, 1)
            pool.wait_ge(s_whi, 2)
            nc.gpsimd.tensor_tensor(wvlo[:, :], wvraw[:, :], wvhi[:, :].bitcast(F32), ALU.subtract).then_inc(s_wlo, 1)

        def att_act(act):
            for g in range(2):
                high_act(act, norms[1], g)

            def values(unit):
                t, half = divmod(unit, 2)
                act.wait_ge(s_v, unit + 1)
                nc.scalar.activation(V[:, t, half * 512:(half + 1) * 512], bank(V_BANKS[unit % 4]),
                                     ACT.Copy).then_inc(s_va, 1)

            for n, (what, hg, g) in enumerate(UNITS):
                act.wait_ge(s_qk, n + 1)
                if n >= 4:
                    act.wait_ge(s_st[n % 4], 32 * (n // 4))
                nc.scalar.activation(sthi[:, n % 4, :], bank(2 + n % 2), ACT.Copy,
                                     scale=(SCALE, 1.0)[what]).then_inc(s_qkhi, 1)
                values(n)
                if n % 4 == 1 and g < 2:
                    high_act(act, norms[1], g + 2)
            for unit in range(len(UNITS), 2 * NT):
                values(unit)
            nc.scalar.activation(mark[:, 12:13], ident[:, 0:1], ACT.Copy).then_inc(s_exp, EXP0)

            def exps(i, b, s):
                at = placed(i, b, s)
                if at:
                    i1, b1, s1 = at
                    c = s1 % 8
                    act.wait_ge(s_max, step(i1, b1, s1 + 1))
                    if is_whole(s1):
                        wait_slot(act, i1, b1, s1)
                        e = efn[:, slot_of(s1), :]
                    else:
                        act.wait_ge(s_lo, nth(i1, b1, s1) + 1)
                        e = ef[:, slot_of(s1), :]
                    nc.scalar.activation(e, bank(2 * ring_slot(s1), 2), ACT.Exp, bias=nmax[:, c:c + 1],
                                         accum_out=esum[:, c:c + 1]).then_inc(s_exp, 1)
                if s > 0 and not is_whole(s - 1):
                    i1, b1, s1 = placed(i, b, s - 1)
                    act.wait_ge(s_exp, step(i1, b1, s1 + (1 + EXP0)))
                    wait_slot(act, i1, b1, s1)
                    n = slot_of(s1)
                    nc.scalar.activation(ehi[:, n, :], ef[:, n, :], ACT.Copy).then_inc(s_hi, 1)

            exps(0, 0, 0)
            for u in range(4):
                act.wait_ge(s_st[u], 32 * len(UNITS) // 4)

            def body(i, b):
                for s in range(STEPS):
                    exps(i, b, s + 1)
            for b in range(B):
                quads(act, b, body)

        def att_dve(dve):
            n = norms[1]
            statistics_dve(dve, n, 0)
            statistics_dve(dve, n, 1)
            scaled_dve(dve, n, 0)
            statistics_dve(dve, n, 2)
            scaled_dve(dve, n, 1)
            low_dve(dve, n, 0)
            statistics_dve(dve, n, 3)
            low_dve(dve, n, 1)
            scaled_dve(dve, n, 2)
            for u, (what, hg, g) in enumerate(UNITS):
                dve.wait_ge(s_qkhi, u + 1)
                nc.vector.scalar_tensor_tensor(stlo[:, u % 4, :], bank(2 + u % 2), (SCALE, 1.0)[what],
                                               sthi[:, u % 4, :].bitcast(F32), ALU.mult,
                                               ALU.subtract).then_inc(s_qklo, 1)
                if u == 1:
                    scaled_dve(dve, n, 3)
                if u % 4 == 2 and g < 2:
                    low_dve(dve, n, g + 2)
            nc.vector.memset(mark[:, 8:9], 0.0).then_inc(s_av, AV0)
            nc.vector.memset(mark[:, 9:10], 0.0).then_inc(s_lo, LO0)
            nc.vector.memset(mark[:, 10:11], 0.0).then_inc(s_op, OP0)
            nc.vector.memset(mark[:, 11:12], 0.0).then_inc(s_o, O0)
            nc.vector.memset(mark[:, 13:14], 0.0).then_inc(s_sum, SUM0)

            def front(i, b, s):
                at = placed(i, b, s)
                if at:
                    i1, b1, s1 = at
                    dve.wait_ge(s_s, step(i1, b1, s1 + 1))
                    nc.vector.tensor_reduce(nmax[:, s1 % 8:s1 % 8 + 1], bank(2 * ring_slot(s1), 2), AX.X, ALU.max,
                                            negate=True).then_inc(s_max, 1)

                def values(i, b, s):
                    h = s // MT
                    return vq[:, h // 2 % 2, s % MT, h % 2 * VD:(h % 2 + 1) * VD]

                one = placed(i, b, s - 1) if s >= 1 else None
                two = placed(i, b, s - 2) if s >= 2 else None
                if one:
                    i1, b1, s1 = one
                    c = s1 % 8
                    dve.wait_ge(s_exp, step(i1, b1, s1 + (1 + EXP0)))
                    nc.vector.reciprocal(rsum[:, c:c + 1], esum[:, c:c + 1]).then_inc(s_rs, 1)
                if two and not is_whole(two[2]):
                    i2, b2, s2 = two
                    c, n = s2 % 8, slot_of(s2)
                    dve.wait_ge(s_vsh, nth(i2, b2, s2) + 1)
                    nc.vector.scalar_tensor_tensor(vs[:, n, VD:2 * VD], values(i2, b2, s2), rsum[:, c:c + 1],
                                                   vs[:, n, 0:VD].bitcast(F32), ALU.mult,
                                                   ALU.subtract).then_inc(s_vsl, 1)
                if one:
                    c = s1 % 8
                    wait_slot(dve, i1, b1, s1)
                    dve.wait_ge(s_rs, step(i1, b1, s1 + 1))
                    if s1 % PST == 0:
                        p1 = s1 // PST
                        dve.wait_ge(s_vq[p1 % 2], i1 * 16 + (b1 * QUADS + p1 // 2 + 1) * 16)
                    if is_whole(s1):
                        dst, done = vsn[:, slot_of(s1), :], s_vsn
                    else:
                        dst, done = vs[:, slot_of(s1), 0:VD], s_vsh
                    nc.vector.tensor_scalar(dst, values(i1, b1, s1), rsum[:, c:c + 1], None,
                                            ALU.mult).then_inc(done, 1)

            AHEAD = 5

            def dve_step(i, b, s, out):
                if s % MT > 1:
                    front(i, b, s + AHEAD)
                if s % MT == MT - 1:
                    at = placed(i, b, s)
                    if at:
                        i1, b1, s1 = at
                        h = s1 // MT
                        dve.wait_ge(s_op, out_number(i1, b1, (h // 2 * 2 + 4 - QUAD) * MT - 1) + (1 + OP0))
                        for half in range(2):
                            if half == 0:
                                dve.wait_ge(s_avh, head(i1, b1, h + 1))
                            else:
                                dve.wait_ge(s_av, step(i1, b1, s1 + (1 + AV0)))
                            nc.vector.tensor_copy(oT[:, h % QUAD, half * 512:(half + 1) * 512],
                                                  bank(6 + half)).then_inc(s_o, 1)
                    for k in range(2):
                        front(i, b, s + AHEAD + 1 + k)
                    if out:
                        n, half = out_number(i, b, s), ((s + 1) // MT - 3) % 2
                        dve.wait_ge(s_op, n + (1 + OP0))
                        dve.wait_ge(s_sum, n + SUM0)
                        a = aT[:, b * N + half * 512:b * N + (half + 1) * 512]
                        nc.vector.tensor_tensor(a, a, bank(out_bank(i, b, s)), ALU.add).then_inc(s_sum, 1)

            for s in range(AHEAD + 2):
                front(0, 0, s)
            for s in range(2 * MT):
                dve_step(0, 0, s, False)

            def body(i, b):
                last = isinstance(i, int) and b == B - 1
                for s in ROTATED:
                    if last and s == STEPS - 1:
                        for g in range(2):
                            statistics_dve(dve, norms[2], g)
                    if last and s == STEPS + 2 * MT - 1:
                        for g in range(2):
                            scaled_dve(dve, norms[2], g)
                    dve_step(i, b, s, True)
            dve.wait_ge(s_a0, 1)
            for b in range(B):
                quads(dve, b, body)

        def att_pool(pool):
            nc.gpsimd.memset(aT[:, :], 0.0).then_inc(s_a0, 1)
            for u in range(4):
                pool.wait_ge(s_st[u], 32 * len(UNITS) // 4)

            def body(i, b):
                for s in range(STEPS):
                    if not is_whole(s):
                        n = slot_of(s)
                        pool.wait_ge(s_hi, nth(i, b, s) + 1)
                        wait_slot(pool, i, b, s)
                        nc.gpsimd.tensor_tensor(elo[:, n, :], ef[:, n, :], ehi[:, n, :].bitcast(F32),
                                                ALU.subtract).then_inc(s_lo, 1)
            for b in range(B):
                quads(pool, b, body)

        block = ctx.enter_context(nc.Block())

        @block.sync
        def _(sp):
            sp.dma_start(xt[:, 0:TPG, :], x_v[0]).then_inc(s_x[0], 16)
            sp.dma_start(consts[:, :], cst).then_inc(s_cst, 16)
            for g in range(1, GR):
                sp.dma_start(xt[:, g * TPG:(g + 1) * TPG, :], x_v[g]).then_inc(s_x[g], 16)
            sp.dma_start(wr_sb[:, :], wr).then_inc(s_cst, 16)
            sp.dma_start(br_sb[:, :], br.unsqueeze(0).broadcast_to([P, E])).then_inc(s_cst, 16)
            sp.dma_start(b2_sb[:, :], b2).then_inc(s_cst, 16)
            first_weights_sync(sp, ffns[0])
            att_weights_sync(sp)
            ffn_sync(sp, ffns[0])
            att_sync(sp)
            for u in range(2):
                sp.wait_ge(s_vq[u], 16 * QUADS * B)
            first_weights_sync(sp, ffns[1])
            sp.wait_ge(s_sum, B * QUADS * OUTS + SUM0)
            for u in range(4):
                sp.wait_ge(s_st[u], 32 * len(UNITS) // 4)
            ffn_sync(sp, ffns[1])
            for g in range(GR):
                sp.wait_ge(norms[3].res, g + 1)
                sp.dma_start(out_v[g], xt[:, g * TPG:(g + 1) * TPG, :]).then_inc(s_out, 16)
            sp.wait_ge(s_out, 16 * GR)
            for F in ffns:
                sp.wait_ge(F.gd, 16)

        @block.gpsimd
        def _(pool):
            nc.gpsimd.memset(mhalf[:, :], -0.5).then_inc(s_fill, 1)
            pool.wait_ge(s_fill, 1)
            nc.gpsimd.memset(ks[:, :, :, :].bitcast(F32), 0.0).then_inc(s_k0, 1)
            norm_pool(pool, norms[0])
            ffn_pool(pool, ffns[0])
            norm_pool(pool, norms[1])
            att_pool(pool)
            first_weights_pool(pool, ffns[1])
            norm_pool(pool, norms[2])
            ffn_pool(pool, ffns[1])

        @block.scalar
        def _(act):
            act.wait_ge(s_cst, 64)
            first_weights_act(act, ffns[0])
            norm_act(act, norms[0])
            att_weights_act(act)
            ffn_act(act, ffns[0])
            att_act(act)
            first_weights_act(act, ffns[1])
            norm_act(act, norms[2])
            ffn_act(act, ffns[1])

        @block.vector
        def _(dve):
            dve.wait_ge(s_cst, 64)
            norm_dve(dve, norms[0])
            ffn_dve(dve, ffns[0])
            att_dve(dve)
            norm_dve(dve, norms[2])
            ffn_dve(dve, ffns[1])
            for g in range(GR):
                residual_dve(dve, norms[3], g)

        @block.tensor
        def _(pe):
            pe.wait_ge(s_cst, 64)
            norm_pe(pe, norms[0], ffns[0])
            ffn_pe(pe, ffns[0])
            att_pe(pe)
            norm_pe(pe, norms[2], ffns[1])
            ffn_pe(pe, ffns[1])


def kernel(L0_attn_x, L0_attn_query_proj, L0_attn_key_proj, L0_attn_value_proj, L0_attn_output_proj,
           L0_ffn_Wr, L0_ffn_br, L0_ffn_W1, L0_ffn_b1, L0_ffn_W2, L0_ffn_b2):
    import numpy as np
    import concourse.bacc as bacc
    from concourse.bass_utils import run_bass_kernel_spmd

    query = np.asarray(L0_attn_query_proj).reshape(KD, H, D).transpose(1, 0, 2)
    key = np.asarray(L0_attn_key_proj)
    consts = np.zeros((P, C_W), np.float32)
    consts[:, C_ID:C_ID + P] = np.eye(P)
    consts[:, C_PRI:] = E - np.arange(E)

    arrays = {
        "x": L0_attn_x,
        "cst": consts,
        "wqk": np.concatenate([query.reshape(H * KD, D), key.reshape(H * KD, D)]).T,
        "wv": np.asarray(L0_attn_value_proj).reshape(H * VD, D).T,
        "wo": np.asarray(L0_attn_output_proj).transpose(1, 2, 0),
        "wr": L0_ffn_Wr,
        "br": L0_ffn_br,
        "w1": L0_ffn_W1,
        "b1": np.asarray(L0_ffn_b1).reshape(E, MC, P).transpose(0, 2, 1),
        "w2": np.asarray(L0_ffn_W2).reshape(E, MC, P, D).transpose(0, 2, 1, 3).reshape(E, P, MC * D),
        "b2": np.asarray(L0_ffn_b2).T,
    }
    nc = bacc.Bacc("TRN2", target_bir_lowering=False, num_devices=1)
    feed, args = {}, []
    for name, a in arrays.items():
        a = np.ascontiguousarray(a)
        feed[f"in_{name}"] = a
        args.append(nc.dram_tensor(f"in_{name}", a.shape, F32, kind="ExternalInput").ap())
    args.append(nc.dram_tensor("out_0", (B, N, D), F32, kind="ExternalOutput").ap())
    macaron_kernel(nc, *args)
    return run_bass_kernel_spmd(nc, [feed], core_ids=[0]).results[0]["out_0"]
```
